# Optimizing a Trainium2 kernel written in Bass

```python
import numpy as np
import jax
import jax.numpy as jnp

def _softmax(x, axis=-1):
    return jax.nn.softmax(x, axis=axis)

def _gelu(x):
    return jax.nn.gelu(x, approximate=True)

def _silu(x):
    return jax.nn.silu(x)

def _sigmoid(x):
    return jax.nn.sigmoid(x)

def _layernorm(x, axis=-1, eps=1e-05):
    m = jnp.mean(x, axis=axis, keepdims=True)
    v = jnp.var(x, axis=axis, keepdims=True)
    return (x - m) / jnp.sqrt(v + eps)

def _scatter_add(tgt, idx, src, axis=0):
    return tgt.at[idx].add(src)

def _segment_sum(src, seg, n):
    return jax.ops.segment_sum(src, seg, n)
kernel_name = 'mk_metaformer_d1_conv_nchw128_r2_27ddea'

def setup_inputs(seed: int=0):
    np.random.seed(seed)
    _w = jnp.asarray

    def _rec_inputs():
        import jax
        import jax.numpy as jnp
        _gk = jax.random.key(seed)
        x = -7.109e-05 + 0.9999 * jax.random.normal(jax.random.fold_in(_gk, 1), (8, 64, 128, 128), jnp.float32)
        return x
    x = _rec_inputs()

    def _L0_conv_setup():
        import jax, jax.numpy as jnp
        import numpy as np
        C = 64
        GROUPS = 8
        EPS = 1e-05
        key = jax.random.key(seed)
        ks = jax.random.split(key, 7)
        x = jax.random.normal(ks[0], (8, C, 128, 128), dtype=jnp.float32)
        gn_w = jax.random.normal(ks[1], (C,), dtype=jnp.float32) * 0.02 + 1.0
        gn_b = jax.random.normal(ks[2], (C,), dtype=jnp.float32) * 0.02
        w1 = jax.random.normal(ks[3], (C, C), dtype=jnp.float32) * (1.0 / np.sqrt(C))
        b1 = jax.random.normal(ks[4], (C,), dtype=jnp.float32) * 0.02
        w2 = jax.random.normal(ks[5], (C, C), dtype=jnp.float32) * (1.0 / np.sqrt(C))
        b2 = jax.random.normal(ks[6], (C,), dtype=jnp.float32) * 0.02
        return {'x': x, 'gn_w': gn_w, 'gn_b': gn_b, 'w1': w1, 'b1': b1, 'w2': w2, 'b2': b2}
    _L0_conv_all = _L0_conv_setup()
    _L0_conv_in = {k: v for k, v in _L0_conv_all.items() if k in ('gn_w', 'gn_b', 'w1', 'b1', 'w2', 'b2')}
    del _L0_conv_all

    def _L0_ffn_setup():
        import jax, jax.numpy as jnp
        import numpy as np
        B, S, D, E, H, O, K = (256, 1024, 64, 32, 256, 64, 8)
        key = jax.random.key(seed)
        k0, k1, k2, k3 = jax.random.split(key, 4)
        x = jax.random.normal(k0, (B, S, D), dtype=jnp.float32)
        gate_w = jax.random.normal(k1, (E, D), dtype=jnp.float32) * (1.0 / np.sqrt(D))
        gate_b = jnp.zeros((E,), dtype=jnp.float32)
        weight1 = jax.random.uniform(k2, (E, D + 1, H), dtype=jnp.float32, minval=-1.0, maxval=1.0) * (1.0 / np.sqrt(D + 1))
        weight2 = jax.random.uniform(k3, (E, H + 1, O), dtype=jnp.float32, minval=-1.0, maxval=1.0) * (1.0 / np.sqrt(H + 1))
        return {'x': x, 'gate_w': gate_w, 'gate_b': gate_b, 'weight1': weight1, 'weight2': weight2}
    _L0_ffn_all = _L0_ffn_setup()
    _L0_ffn_in = {k: v for k, v in _L0_ffn_all.items() if k in ('gate_w', 'gate_b', 'weight1', 'weight2')}
    del _L0_ffn_all
    return {'x': x, 'L0_conv_gn_w': _L0_conv_in['gn_w'], 'L0_conv_gn_b': _L0_conv_in['gn_b'], 'L0_conv_w1': _L0_conv_in['w1'], 'L0_conv_b1': _L0_conv_in['b1'], 'L0_conv_w2': _L0_conv_in['w2'], 'L0_conv_b2': _L0_conv_in['b2'], 'L0_ffn_gate_w': _L0_ffn_in['gate_w'], 'L0_ffn_gate_b': _L0_ffn_in['gate_b'], 'L0_ffn_weight1': _L0_ffn_in['weight1'], 'L0_ffn_weight2': _L0_ffn_in['weight2']}

def reference(x, L0_conv_gn_w, L0_conv_gn_b, L0_conv_w1, L0_conv_b1, L0_conv_w2, L0_conv_b2, L0_ffn_gate_w, L0_ffn_gate_b, L0_ffn_weight1, L0_ffn_weight2):
    import jax
    import jax.numpy as jnp

    def _L0_conv_ref(x, gn_w, gn_b, w1, b1, w2, b2):
        import jax, jax.numpy as jnp
        import numpy as np
        C = 64
        GROUPS = 8
        EPS = 1e-05
        x_ifft = jnp.fft.ifft2(jnp.fft.fft2(x, axes=(-2, -1)), axes=(-2, -1)).real.astype(x.dtype)
        B, Ch, H, W = x_ifft.shape
        g = x_ifft.reshape(B, GROUPS, Ch // GROUPS, H, W)
        mean = g.mean(axis=(2, 3, 4), keepdims=True)
        var = g.var(axis=(2, 3, 4), keepdims=True)
        xn = ((g - mean) * jax.lax.rsqrt(var + EPS)).reshape(B, Ch, H, W)
        xn = xn * gn_w[None, :, None, None] + gn_b[None, :, None, None]
        h = jnp.einsum('oc,bchw->bohw', w1, xn) + b1[None, :, None, None]
        h = jax.nn.relu(h)
        ffn = jnp.einsum('oc,bchw->bohw', w2, h) + b2[None, :, None, None]
        return x_ifft + ffn

    def _L0_ffn_ref(x, gate_w, gate_b, weight1, weight2):
        import jax, jax.numpy as jnp
        import numpy as np
        B, S, D, E, H, O, K = (256, 1024, 64, 32, 256, 64, 8)
        Bn, Sn, Dn = x.shape
        logits = jnp.einsum('bsd,ed->bse', x, gate_w) + gate_b
        probs = jax.nn.softmax(logits, axis=1)
        vals, idx = jax.lax.top_k(probs.transpose(0, 2, 1), K)
        topv = vals.transpose(0, 2, 1)
        topi = idx.transpose(0, 2, 1)
        flat_idx = topi.reshape(Bn, K * E)
        gathered = jnp.take_along_axis(x, flat_idx[:, :, None], axis=1)
        gathered = gathered.reshape(Bn, K, E, Dn)
        pooled = jnp.einsum('bked,bke->bed', gathered, topv)
        ones = jnp.ones((E, Bn, 1), dtype=x.dtype)
        h = jnp.concatenate([pooled.transpose(1, 0, 2), ones], axis=-1)
        h = jax.nn.gelu(jnp.einsum('ebd,edh->ebh', h, weight1), approximate=False)
        h = jnp.concatenate([h, ones], axis=-1)
        out = jnp.einsum('ebh,eho->ebo', h, weight2)
        out = out.transpose(1, 0, 2)
        weighted = jnp.einsum('beo,bke->bkeo', out, topv).reshape(Bn, K * E, O)
        outputs = jnp.zeros((Bn, Sn, O), dtype=x.dtype)
        outputs = outputs.at[jnp.arange(Bn)[:, None], flat_idx].add(weighted)
        return outputs

    def _gn(v, G=32, eps=1e-05):
        B_, C_, H_, W_ = v.shape
        g = v.reshape(B_, G, C_ // G, H_, W_)
        m = jnp.mean(g, axis=(2, 3, 4), keepdims=True)
        s = jnp.var(g, axis=(2, 3, 4), keepdims=True)
        return ((g - m) / jnp.sqrt(s + eps)).reshape(v.shape)

    def _ln_c(v, eps=1e-06):
        m = jnp.mean(v, axis=1, keepdims=True)
        s = jnp.var(v, axis=1, keepdims=True)
        return (v - m) / jnp.sqrt(s + eps)

    def _ln_t(v, eps=1e-05):
        m = jnp.mean(v, axis=-1, keepdims=True)
        s = jnp.var(v, axis=-1, keepdims=True)
        return (v - m) / jnp.sqrt(s + eps)

    def _to_tokens(v):
        B_, C_, H_, W_ = v.shape
        return v.reshape(B_, C_, H_ * W_).transpose(0, 2, 1)

    def _from_tokens(t, like):
        B_, C_, H_, W_ = like.shape
        return t.transpose(0, 2, 1).reshape(B_, C_, H_, W_)
    x = x + _L0_conv_ref(_ln_c(x), L0_conv_gn_w, L0_conv_gn_b, L0_conv_w1, L0_conv_b1, L0_conv_w2, L0_conv_b2)
    t = _to_tokens(x)
    t = t + _L0_ffn_ref(_ln_t(t), L0_ffn_gate_w, L0_ffn_gate_b, L0_ffn_weight1, L0_ffn_weight2)
    x = _from_tokens(t, x)
    return x

_drawn_inputs = setup_inputs


def setup_inputs(seed=0):
    import zlib

    import numpy as np

    out = dict(_drawn_inputs(seed))
    spreads = {'L0_ffn_gate_b': (0.0, 0.8)}
    factors = {'L0_conv_gn_w': 7.238,
     'L0_conv_gn_b': 8.0,
     'L0_conv_b1': 21.524,
     'L0_conv_b2': 5.331,
     'L0_ffn_gate_w': 8.0,
     'L0_ffn_weight1': 8.0,
     'L0_ffn_weight2': 8.0}
    for name, (base, spread) in spreads.items():
        noise = np.random.default_rng([zlib.crc32(name.encode()), seed]).standard_normal(out[name].shape)
        drawn = base * np.exp(spread * noise) if base else spread * noise
        out[name] = jnp.asarray(drawn.astype(out[name].dtype))
    for name, factor in factors.items():
        out[name] = (out[name] * factor).astype(out[name].dtype)
    return out
```

```python
from contextlib import ExitStack

import concourse.bass as bass
from concourse import mybir

F32 = mybir.dt.float32
F32R = mybir.dt.float32r
U32 = mybir.dt.uint32
ALU = mybir.AluOpType
ACT = mybir.ActivationFunctionType
AX = mybir.AxisListType

P = 128
C = 64
HALVES = 2
NB = 8
PIX = 128 * 128
HW = PIX // HALVES
CH = 512
SUB = 256
NCH = HW // CH
GRP = 4
NG = NCH // GRP
NE = 32
K = 8
HID = 256
EPS_C = 1e-6
EPS = 1e-5
GN_GROUP = 8
GATHERS = K * NE // P
MRG = K + K + 1

MEAN_AT, XC_AT, RSTD_AT, U_AT, GN_AT, MERGE_AT = 3, 4, 8, 9, 13, 9
STEPS = NCH + 1


def chunk_of(s):
    return GRP * (s % GRP) + s // GRP


def mk_metaformer_kernel(nc, x, gn_w, gn_b, w1T, b1, w2T, b2, gateT, gate_b, e_w1, e_w2, out):
    ctx = ExitStack()
    with ctx:
        def sb(name, shape, dt=F32):
            return ctx.enter_context(nc.sbuf_tensor(name, shape, dt))

        def bank(name):
            return ctx.enter_context(nc.psum_tensor(name, [P, CH], F32))

        def sem(name):
            return ctx.enter_context(nc.semaphore(name))

        xs = [sb(f"xs{i}", [P, HW]) for i in range(2)]
        us = [sb(f"us{i}", [P, HW]) for i in range(2)]
        lg = [sb(f"lg{i}", [P, HW // 2]) for i in range(2)]
        hid = [sb(f"hid{i}", [P, CH]) for i in range(2)]
        tok = [sb(f"tok{i}", [P, HALVES, GRP, C]) for i in range(2)]
        sqc = sb("sqc", [P, GRP, CH])
        sqx = sb("sqx", [P, GRP, CH])
        junk = sb("junk", [P, 2, CH], mybir.dt.bfloat16)

        ident = sb("ident", [P, P])
        stat_w = sb("stat_w", [P, 8, 32])
        spread = sb("spread", [P, 16 * 64], F32R)
        second = sb("second", [P, 1])
        gsel = sb("gsel", [P, P])
        w1bd = sb("w1bd", [P, P])
        w1n = sb("w1n", [P, P])
        cen = w1n
        w2bd = sb("w2bd", [P, P])
        gbd = sb("gbd", [P, C])
        gcen = sb("gcen", [P, C])
        vecs = sb("vecs", [P, 4])
        gate_bias = sb("gate_bias", [NE, 1])
        ones = junk[:, 0, 0:2 * P].bitcast(F32)
        kmask = sb("kmask", [P, 4])
        esel = sb("esel", [P, NE])
        rep = sb("rep", [NE, P])
        iota32 = sb("iota32", [NE, 32])
        rowoff = sb("rowoff", [P, 1])

        hi = sb("hi", [P, SUB], F32R)
        mean_s = sb("mean_s", [P, SUB], F32R)
        rstd_s = sb("rstd_s", [P, SUB], F32R)
        rstd2_s = sb("rstd2_s", [P, SUB], F32R)
        lnv, y0, ta, tb = (sb(n, [P, SUB]) for n in ("lnv", "y0", "ta", "tb"))
        v2, y2 = lnv, y0
        gsum = sb("gsum", [P, NCH])
        gsq = sb("gsq", [P, NCH])
        gs = sb("gs", [P, 2])
        gt = sb("gt", [P, 12])
        b1n = sb("b1n", [P, 1])
        spare = sb("spare", [P, 2])

        cnd = sb("cnd", [P, MRG])
        top_i = sb("top_i", [P, K], U32)
        top_hi = sb("top_hi", [P, K], U32)
        nmax = sb("nmax", [P, 1])
        cval = sb("cval", [NE, 4 * K])
        cpix = sb("cpix", [NE, 4 * K])
        csum = sb("csum", [NE, 4])
        fval = sb("fval", [NE, K])
        fpos = sb("fpos", [NE, K], U32)
        fposf = sb("fposf", [NE, K])
        onehot = sb("onehot", [NE, K, 32])
        gbm = sb("gbm", [NE, 4])
        tval = sb("tval", [NE, K])
        dexp = sb("dexp", [NE, 4])
        djunk = sb("djunk", [NE, 4])
        pv = sb("pv", [NE, 2 * K])
        pvm = sb("pvm", [P, 2 * GATHERS, 4])
        pvt = sb("pvt", [P, 2 * GATHERS])
        offs = sb("offs", [P, 1])
        idxf = sb("idxf", [P, GATHERS])
        idx_all = sb("idx_all", [P, NB, GATHERS], U32)
        px_all = sb("px_all", [P, NB, GATHERS])
        tv_all = sb("tv_all", [P, NB, GATHERS])
        rows_all = sqx[:].rearrange("p g n -> p (g n)")[:, 0:NB * GATHERS * C].rearrange(
            "p (b g c) -> p b g c", b=NB, g=GATHERS)
        zs = sqc[:].rearrange("p g n -> p (g n)")[:, 2 * CH:4 * CH].rearrange(
            "p (b g c) -> p b g c", b=NB, g=GATHERS)
        tr = sb("tr", [P, 6, NB * GATHERS])
        z = sb("z", [P, GATHERS, C])
        pooled = sb("pooled", [C + 1, NE, NB])

        bc = [bank(f"bc{i}") for i in range(2)]
        pc, pd, pe_b, pt = bank("pc"), bank("pd"), bank("pe_b"), bank("pt")
        st1, st2 = bank("st1"), bank("st2")
        lgp = pe_b[:, 0:SUB]
        mrg_p = st1[0:NE, 0:4 * MRG]
        rep_p = st1[:, 80:80 + 2 * K]
        gn_p = st1[:, 140:142]
        gnb_p = st1[:, 144:145]

        w_in, x_in = sem("w_in"), [sem(f"x_in{m}") for m in range(NG)]
        const_p, const_v, const_d, const_t = sem("const_p"), sem("const_v"), sem("const_d"), sem("const_t")
        sumx_done, mean_ready, mean_steps = sem("sumx_done"), sem("mean_ready"), sem("mean_steps")
        bcm_done, xc_done, sqc_done, sumsq_done = (sem(n) for n in ("bcm_done", "xc_done", "sqc_done", "sumsq_done"))
        lnv_done, y0_ready, rstd_steps, rstd_ready = (sem(n) for n in ("lnv_done", "y0_ready", "rstd_steps", "rstd_ready"))
        bcr_done, u_done, usq_done, s_done = (sem(n) for n in ("bcr_done", "u_done", "usq_done", "s_done"))
        gn_steps, gnred_ready, gnps_done, gnv_ready = (sem(n) for n in ("gn_steps", "gnred_ready", "gnps_done", "gnv_ready"))
        gnln_done, gny_ready, gnbias_ready, w1n_ready = (sem(n) for n in ("gnln_done", "gny_ready", "gnbias_ready", "w1n_ready"))
        c_done, h_done, d_done, x1_done = (sem(n) for n in ("c_done", "h_done", "d_done", "x1_done"))
        e_done, lcopy_done, t_done, tok_done = (sem(n) for n in ("e_done", "lcopy_done", "t_done", "tok_done"))
        sqx_done, grp_done = sem("sqx_done"), sem("grp_done")
        stored = [sem(f"stored{i}") for i in range(2)]
        msq_done, var2_ready, ln2_done, y2_ready = (sem(n) for n in ("msq_done", "var2_ready", "ln2_done", "y2_ready"))
        tail_steps, rstd2_ready, bcl_done, l_done = (sem(n) for n in ("tail_steps", "rstd2_ready", "bcl_done", "l_done"))
        top_ready, expl_done, mrg_done, bias_ready = (sem(n) for n in ("top_ready", "expl_done", "mrg_done", "bias_ready"))
        tval_done, pv_ready, rep_done, idx_ready = (sem(n) for n in ("tval_done", "pv_ready", "rep_done", "idx_ready"))
        rows_in = [sem("rows_in0"), sem("rows_in1")]
        ln_steps, rvar_ready, rln_done, ry_ready = (sem(n) for n in ("ln_steps", "rvar_ready", "rln_done", "ry_ready"))
        z_ready, pool_done, pooled_ready = (sem(n) for n in ("z_ready", "pool_done", "pooled_ready"))
        ew_in, l1_done, gelu_done, l2_done = (sem(n) for n in ("ew_in", "l1_done", "gelu_done", "l2_done"))
        eo_ready, ob_done, diag_ready = (sem(n) for n in ("eo_ready", "ob_done", "diag_ready"))
        pxr_done, eq_ready, add_done, row_ready, scattered = (
            sem(n) for n in ("pxr_done", "eq_ready", "add_done", "row_ready", "scattered"))
        pex_done, ebias_ready = sem("pex_done"), sem("ebias_ready")
        pool_steps, const_steps = sem("pool_steps"), sem("const_steps")

        x_h = x.rearrange("b c (h m q n) -> b h c m q n", h=HALVES, m=GRP, q=NG)
        out_t = out.rearrange("b (h j p t) c -> b j p h (t c)", h=HALVES, j=NCH, p=P)
        out_rows = out.rearrange("b p c -> (b p) c")

        MEAN_STEPS, RSTD_STEPS, GN_STEPS, TAIL_STEPS = 1, 4, 12, 27
        CONST_P, CONST_V = 1, 1

        def chunk(buf, s):
            j = chunk_of(s)
            return buf[:, CH * j:CH * (j + 1)]

        def wait(eng, s, value):
            if not isinstance(value, int) or value > 0:
                eng.wait_ge(s, value)

        def hold(eng, cell):
            eng.tensor_tensor(cell, second[:, 0:1], second[:, 0:1], ALU.mult)

        class Steps:
            def __init__(self, eng, s, base):
                self.eng, self.sem, self.base, self.n = eng, s, base, 0

            def __call__(self, ins):
                self.n += 1
                ins.then_inc(self.sem, 1)
                self.eng.wait_ge(self.sem, self.base + self.n)

        def newton(link, v, y, a, eps):
            link(nc.vector.scalar_tensor_tensor(out=a, in0=v, scalar=eps, in1=y, op0=ALU.add, op1=ALU.mult))
            link(nc.vector.scalar_tensor_tensor(out=a, in0=a, scalar=-0.5, in1=y, op0=ALU.mult, op1=ALU.mult))

        block = ctx.enter_context(nc.Block())

        @block.sync
        def _(sp):
            def load(b, m, slot):
                for h in range(HALVES):
                    dst = xs[slot][C * h:C * h + C, :].rearrange("c (k q n) -> c k q n", k=GRP, q=NG)[:, :, m, :]
                    src = x_h[b, h, :, :, m, :] if isinstance(b, int) else \
                        x_h[bass.ds(b, 1), h, :, :, m, :].rearrange("a c m n -> (a c) m n")
                    sp.dma_start(dst, src).then_inc(x_in[m], 16)

            for m in range(NG):
                load(0, m, 0)
            for vec, src in enumerate((gn_w, gn_b, b1, b2)):
                for h in range(HALVES):
                    sp.dma_start(vecs[C * h:C * h + C, vec:vec + 1], src.rearrange("(c a) -> c a", a=1)).then_inc(w_in, 16)
            sp.dma_start(gate_bias[:], gate_b.rearrange("(e a) -> e a", a=1)).then_inc(w_in, 16)
            sp.wait_ge(const_d, 1)
            for h in range(HALVES):
                r = slice(C * h, C * h + C)
                sp.dma_start(w1bd[r, r], w1T).then_inc(w_in, 16)
                sp.dma_start(w2bd[r, r], w2T).then_inc(w_in, 16)
                sp.dma_start(gbd[r, NE * h:NE * h + NE], gateT).then_inc(w_in, 16)
            for m in range(NG):
                load(1, m, 1)

            def iteration(it, par, loads):
                for s in range(NCH + 1):
                    if s < NCH:
                        sp.wait_ge(tok_done, it * NCH + s + 1)
                        dst = out_t[it, chunk_of(s)] if isinstance(it, int) else \
                            out_t[bass.ds(it, 1), chunk_of(s)].rearrange("a p h n -> (a p) h n")
                        sp.dma_start(dst, tok[s % 2][:].rearrange("p h t c -> p h (t c)")).then_inc(stored[s % 2], 16)
                    if loads and s >= GRP and s % GRP == 0:
                        sp.wait_ge(grp_done, it * NG + s // GRP)
                        load(it + 2, s // GRP - 1, par)

            iteration(0, 0, True)
            with sp.Fori(0, 2) as i:
                iteration(2 * i + 1, 1, True)
                iteration(2 * i + 2, 0, True)
            iteration(5, 1, True)
            iteration(6, 0, False)
            sp.wait_ge(grp_done, 7 * NG)
            sp.dma_start(us[0][0:C + 1, :].rearrange("d (e n) -> d e n", e=NE),
                         e_w1.rearrange("e d n -> d e n")).then_inc(ew_in, 16)
            for k in range(2):
                sp.dma_start(xs[0][:, 0:NE * 2 * C].rearrange("p (e k o) -> p e k o", e=NE, k=2)[:, :, k, :],
                             e_w2[:, k * P:(k + 1) * P, :].rearrange("e p o -> p e o")).then_inc(ew_in, 16)
            sp.dma_start(xs[0][0:NE, NE * 2 * C:NE * 2 * C + C], e_w2[:, HID, :]).then_inc(ew_in, 16)
            iteration(7, 1, False)

        @block.tensor
        def _(pe):
            def sub_sum(dst, src, s, sub, start):
                c, q = s % GRP, 2 * (s // GRP) + sub
                col = CH * chunk_of(s) if src.shape[-1] == HW else CH * (s % GRP)
                return pe.matmul(dst[32 * c:32 * c + 32], stat_w[:, q, :], src[:, col + SUB * sub:col + SUB * sub + SUB],
                                 start=start, stop=True, skip_group_check=True)

            def sum_group(dst, src, m, first):
                for sub in range(2):
                    for c in range(GRP):
                        mm = sub_sum(dst, src, GRP * m + c, sub, first and m == 0 and sub == 0)
                return mm

            def spread_chunk(dst, stat, j):
                c = j // GRP
                for sub in range(2):
                    w = 2 * C * (2 * (j % GRP) + sub)
                    mm = pe.matmul(dst[:, SUB * sub:SUB * sub + SUB], spread[32 * c:32 * c + 32, w:w + 2 * C],
                                   stat[32 * c:32 * c + 32, :], start=True, stop=True)
                return mm

            def iteration(it, par, p1, p2, tl):
                b, n, t = it, it + 1, it - 1
                nxt = 1 - par

                def bcl(i):
                    if i == 0:
                        pe.wait_ge(rstd2_ready, t + 1)
                        wait(pe, u_done, NCH * (min(it + 1, NB) if isinstance(it, int) else it + 1))
                    if i >= 2:
                        pe.wait_ge(l_done, 8 * t + i - 1)
                    for k in range(2):
                        j = 2 * i + k
                        c, w = j // GRP, 4 * C * (j % GRP)
                        mm = pe.matmul(bc[i % 2][:, SUB * k:SUB * k + SUB],
                                       spread[32 * c:32 * c + 32, w:w + 4 * C:2],
                                       rstd2_s[32 * c:32 * c + 32, :], start=True, stop=True)
                    mm.then_inc(bcl_done, 1)

                def bcm(k):
                    if k == 0:
                        pe.wait_ge(mean_ready, n + 1)
                    if k < 2 and tl:
                        pe.wait_ge(l_done, 8 * (t + 1))
                    if k >= 2:
                        pe.wait_ge(xc_done, NCH * n + k - 1)
                    spread_chunk(bc[k % 2], mean_s, chunk_of(k)).then_inc(bcm_done, 1)

                def bcr(k):
                    if k == 0:
                        pe.wait_ge(rstd_ready, n + 1)
                    if k < 2:
                        pe.wait_ge(xc_done, NCH * (n + 1))
                    else:
                        pe.wait_ge(u_done, NCH * n + k - 1)
                    spread_chunk(bc[k % 2], rstd_s, chunk_of(k)).then_inc(bcr_done, 1)

                def conv1(s):
                    if s == 0:
                        pe.wait_ge(w1n_ready, 2 * (b + 1))
                    wait(pe, h_done, NCH * b + s)
                    pe.matmul(pc[:], w1n[:], chunk(us[par], s), start=True, stop=True).then_inc(c_done, 1)

                def conv2(s):
                    pe.wait_ge(h_done, NCH * b + s + 1)
                    wait(pe, x1_done, NCH * b + s)
                    pe.matmul(pd[:], w2bd[:], hid[s % 2][:], start=True, stop=True).then_inc(d_done, 1)

                def logits_and_tokens(s):
                    pe.wait_ge(x1_done, NCH * b + s + 1)
                    wait(pe, lcopy_done, NCH * b + s)
                    col = CH * chunk_of(s)
                    for slot in range(2):
                        mm = pe.matmul(lgp[C * slot:C * slot + C], gcen[:],
                                       xs[par][:, col + SUB * slot:col + SUB * slot + SUB], start=True, stop=True)
                    mm.then_inc(e_done, 1)
                    wait(pe, tok_done, NCH * b + s)
                    for k in range(4):
                        mm = pe.transpose(pt[:, P * k:P * k + P], xs[par][:, col + k:col + CH:4], ident[:])
                    mm.then_inc(t_done, 1)

                for s in range(STEPS):
                    fill = []
                    if p1 and XC_AT <= s < XC_AT + NG:
                        fill = [(bcm, GRP * (s - XC_AT) + k) for k in range(GRP)]
                    if p1 and U_AT <= s < U_AT + NG:
                        fill = [(bcr, GRP * (s - U_AT) + k) for k in range(GRP)]
                    if tl and s in (1, 2):
                        fill = [(bcl, 4 * (s - 1) + k) for k in range(4)]
                    if p2 and s == 0:
                        conv1(0)
                    if p1 and XC_AT < s <= XC_AT + NG:
                        m = s - XC_AT - 1
                        pe.wait_ge(sqc_done, NCH * n + GRP * (m + 1))
                        sum_group(st1[:, SUB:2 * SUB], sqc[:].rearrange("p g n -> p (g n)"), m, True).then_inc(sumsq_done, 1)
                    if p2 and s + 1 < NCH:
                        conv1(s + 1)
                    for f, a in fill[0:1]:
                        f(a)
                    if p2 and s < NCH:
                        conv2(s)
                    for f, a in fill[1:3]:
                        f(a)
                    if p2 and s >= 1:
                        logits_and_tokens(s - 1)
                    for f, a in fill[3:]:
                        f(a)
                    if p2 and s >= GRP and s % GRP == 0:
                        m = s // GRP - 1
                        if m == 0 and tl:
                            pe.wait_ge(var2_ready, t + 1)
                        sum_group(st2[:, 0:SUB], xs[par][:], m, True)
                        pe.wait_ge(sqx_done, NCH * b + GRP * (m + 1))
                        sum_group(st2[:, SUB:2 * SUB], sqx[:].rearrange("p g n -> p (g n)"), m, False).then_inc(grp_done, 1)
                    if p1 and s == MEAN_AT:
                        wait(pe, w1n_ready, 2 * n)
                        for m in range(NG):
                            pe.wait_ge(x_in[m], 32 * (n + 1))
                            mm = sum_group(st1[:, 0:SUB], xs[nxt][:], m, True)
                        mm.then_inc(sumx_done, 1)
                    if tl and s == MERGE_AT:
                        pe.wait_ge(top_ready, t + 1)
                        pe.wait_ge(expl_done, t + 1)
                        for r in range(4):
                            mm = pe.matmul(mrg_p[:, MRG * r:MRG * r + MRG], ident[:, NE * r:NE * r + NE], cnd[:],
                                           start=True, stop=True)
                        mm.then_inc(mrg_done, 1)
                    if tl and s == MERGE_AT + 2:
                        pe.wait_ge(pv_ready, t + 1)
                        pe.matmul(rep_p, rep[:], pv[:],
                                  start=True, stop=True).then_inc(rep_done, 1)
                    if p1 and s == GN_AT + 1:
                        if tl:
                            pe.wait_ge(idx_ready, t + 1)
                        pe.wait_ge(gnred_ready, 2 * (n + 1))
                        pe.matmul(gn_p, gsel[:], gs[:], start=True, stop=True).then_inc(gnps_done, 1)
                    if p1 and s == GN_AT + 2:
                        pe.wait_ge(gnbias_ready, n + 1)
                        pe.matmul(gnb_p, w1bd[:], gt[:, 7:8], start=True, stop=True).then_inc(gnps_done, 1)

            pe.wait_ge(const_v, CONST_V)
            pe.wait_ge(w_in, 16 * 15)
            pe.matmul(pe_b[:, 0:C], cen[:], gbd[:], start=True, stop=True).then_inc(const_t, 1)
            pe.wait_ge(const_v, CONST_V + 1)
            iteration(-1, 1, True, False, False)
            iteration(0, 0, True, True, False)
            with pe.Fori(0, 3) as i:
                iteration(2 * i + 1, 1, True, True, True)
                iteration(2 * i + 2, 0, True, True, True)
            iteration(7, 1, False, True, True)
            iteration(8, 0, False, False, True)

            ew1 = us[0][0:C + 1, :].rearrange("d (e n) -> d e n", e=NE)
            ew2 = xs[0][:, 0:NE * 2 * C].rearrange("p (e k o) -> p e k o", e=NE, k=2)
            eb2 = xs[0][0:NE, NE * 2 * C:NE * 2 * C + C]
            pe.wait_ge(ew_in, 64)
            pe.transpose(pt[0:C, 0:NE], eb2, ident[0:NE, 0:NE]).then_inc(pex_done, 1)
            pe.wait_ge(z_ready, 2)
            for b in range(NB):
                for g in range(GATHERS):
                    mm = pe.matmul(bc[0][0:C, NE * b:NE * b + NE], zs[:, b, g, :], esel[:],
                                   start=(g == 0), stop=(g == GATHERS - 1))
            mm.then_inc(pool_done, 1)
            pe.wait_ge(pooled_ready, 1)
            for e in range(NE):
                for k in range(2):
                    mm = pe.matmul(pc[:, 16 * e + 8 * k:16 * e + 8 * k + 8], ew1[:, e, P * k:P * k + P], pooled[:, e, :],
                                   start=True, stop=True)
            mm.then_inc(l1_done, 1)
            pe.wait_ge(gelu_done, 1)
            for e in range(NE):
                for k in range(2):
                    mm = pe.matmul(pd[0:C, 8 * e:8 * e + 8], ew2[:, e, k, :], hid[0][:, 16 * e + 8 * k:16 * e + 8 * k + 8],
                                   start=(k == 0), stop=(k == 1))
            mm.then_inc(l2_done, 1)
            pe.wait_ge(eo_ready, 1)
            for b in range(NB):
                wait(pe, row_ready, b)
                pe.matmul(pt[:, 0:C], us[1][0:C, P * b:P * b + P], ident[0:C, 0:C],
                          start=True, stop=True).then_inc(ob_done, 1)
                pe.wait_ge(diag_ready, b + 1)
                for g in range(GATHERS):
                    mm = pe.matmul(bc[0][:, P * g:P * g + P], ones, hid[0][:, P * g:P * g + P], start=True, stop=True)
                mm.then_inc(pxr_done, 1)
                pe.wait_ge(eq_ready, b + 1)
                for g in range(GATHERS):
                    for f in range(GATHERS):
                        mm = pe.matmul(bc[1][:, C * g:C * g + C], sqc[:, f, P * g:P * g + P], z[:, f, :],
                                       start=(f == 0), stop=(f == GATHERS - 1))
                mm.then_inc(add_done, 1)

        @block.scalar
        def _(act):
            def rsqrt_start(v, ln, y, eps, ln_done, y_ready, count):
                nc.scalar.activation(ln, v, ACT.Ln, bias=eps).then_inc(ln_done, 1)
                act.wait_ge(ln_done, count)
                nc.scalar.activation(y, ln, ACT.Exp, scale=-0.5).then_inc(y_ready, 1)

            def token_rsqrt(part, b0, b1):
                act.wait_ge(rvar_ready, part + 1)
                n = slice(GATHERS * b0, GATHERS * b1)
                rsqrt_start(tr[:, 1, n], tr[:, 3, n], tr[:, 2, n], 0.0, rln_done, ry_ready, part + 1)

            def iteration(it, par, p1, p2, tl):
                b, n, t = it, it + 1, it - 1
                nxt = 1 - par

                def relu(s):
                    act.wait_ge(c_done, NCH * b + s + 1)
                    wait(act, d_done, NCH * b + s - 1)
                    if s == 0:
                        act.wait_ge(w1n_ready, 2 * (b + 1))
                    nc.scalar.activation(hid[s % 2][:], pc[:], ACT.Relu, bias=b1n[:]).then_inc(h_done, 1)

                def square_xc(k):
                    act.wait_ge(xc_done, NCH * n + k + 1)
                    wait(act, sumsq_done, NG * n + k // GRP)
                    nc.scalar.activation(sqc[:, k % GRP, :], chunk(us[nxt], k), ACT.Square).then_inc(sqc_done, 1)

                def square_u(k):
                    act.wait_ge(u_done, NCH * n + k + 1)
                    wait(act, usq_done, NCH * n + k - 1)
                    if k == 0:
                        wait(act, gnred_ready, 2 * n)
                    nc.scalar.activation(junk[:, k % 2, :], chunk(us[nxt], k), ACT.Square,
                                         accum_out=gsq[:, k:k + 1]).then_inc(usq_done, 1)

                for s in range(STEPS):
                    fill = []
                    if p1 and XC_AT <= s < XC_AT + NG:
                        fill = [(square_xc, GRP * (s - XC_AT) + k) for k in range(GRP)]
                    if p1 and U_AT <= s < U_AT + NG:
                        fill = [(square_u, GRP * (s - U_AT) + k) for k in range(GRP)]
                    if p2 and s == 0:
                        relu(0)
                    if p2 and s + 1 < NCH:
                        relu(s + 1)
                    for f, a in fill[0:2]:
                        f(a)
                    if p2 and s >= 1:
                        act.wait_ge(t_done, NCH * b + s)
                        wait(act, stored[(s - 1) % 2], 16 * (8 * b + (s - 1) // 2))
                        nc.scalar.activation(tok[(s - 1) % 2][:].rearrange("p h t c -> p t h c"),
                                             pt[:].rearrange("p (t h c) -> p t h c", t=4, h=2), ACT.Copy).then_inc(tok_done, 1)
                    for f, a in fill[2:]:
                        f(a)
                    if tl and s == 0:
                        act.wait_ge(grp_done, NG * (t + 1))
                        nc.scalar.activation(ta[:], st2[:, 0:SUB], ACT.Square).then_inc(msq_done, 1)
                        act.wait_ge(var2_ready, t + 1)
                        rsqrt_start(v2[:], ta[:], y2[:], 0.0, ln2_done, y2_ready, t + 1)
                    if tl and s == 3:
                        act.wait_ge(top_ready, t + 1)
                        nc.scalar.activation(lg[nxt][:], lg[nxt][:], ACT.Exp, bias=nmax[:],
                                             accum_out=cnd[:, 2 * K:MRG]).then_inc(expl_done, 1)
                    if tl and not p2 and s == MERGE_AT:
                        token_rsqrt(0, 0, NB - 1)
                    if tl and s == MERGE_AT + 1:
                        act.wait_ge(bias_ready, t + 1)
                        nc.scalar.activation(tval[:], fval[:], ACT.Exp, bias=gbm[:, 1:2]).then_inc(tval_done, 1)
                        nc.scalar.activation(dexp[:], cval[:, 0:4 * K:K], ACT.Exp, bias=gbm[:, 1:2]).then_inc(tval_done, 1)
                    if p1 and s == RSTD_AT:
                        act.wait_ge(sumsq_done, NG * (n + 1))
                        act.wait_ge(const_v, CONST_V)
                        nc.scalar.activation(lnv[:], st1[:, SUB:2 * SUB], ACT.Ln, bias=gt[:, 10:11]).then_inc(lnv_done, 1)
                        act.wait_ge(lnv_done, n + 1)
                        nc.scalar.activation(y0[:], lnv[:], ACT.Exp, scale=-0.5).then_inc(y0_ready, 1)
                    if p1 and s == GN_AT + 1:
                        act.wait_ge(gnv_ready, n + 1)
                        rsqrt_start(gt[:, 3:4], gt[:, 8:9], gt[:, 4:5], 0.0, gnln_done, gny_ready, n + 1)

            iteration(-1, 1, True, False, False)
            iteration(0, 0, True, True, False)
            with act.Fori(0, 3) as i:
                iteration(2 * i + 1, 1, True, True, True)
                iteration(2 * i + 2, 0, True, True, True)
            iteration(7, 1, False, True, True)
            iteration(8, 0, False, False, True)

            token_rsqrt(1, NB - 1, NB)
            act.wait_ge(l1_done, 1)
            nc.scalar.activation(hid[0][:], pc[:], ACT.Gelu).then_inc(gelu_done, 1)

        @block.vector
        def _(dve):
            def iteration(it, par, p1, p2, tl):
                b, n, t = it, it + 1, it - 1
                nxt = 1 - par
                tail = Steps(dve, tail_steps, TAIL_STEPS * t if tl else 0)

                def l_mult(i):
                    dve.wait_ge(bcl_done, 8 * t + i + 1)
                    lt = lg[nxt][:, CH * i:CH * (i + 1)]
                    nc.vector.tensor_tensor(lt, lt, bc[i % 2][:], ALU.mult).then_inc(l_done, 1)

                def centre(k):
                    dve.wait_ge(bcm_done, NCH * n + k + 1)
                    nc.vector.tensor_tensor(chunk(us[nxt], k), chunk(xs[nxt], k), bc[k % 2][:],
                                            ALU.subtract).then_inc(xc_done, 1)

                def scale(k):
                    dve.wait_ge(bcr_done, NCH * n + k + 1)
                    nc.vector.tensor_tensor_reduce(chunk(us[nxt], k), chunk(us[nxt], k), bc[k % 2][:], 1.0, 0.0,
                                                   ALU.mult, ALU.add, gsum[:, k:k + 1]).then_inc(u_done, 1)

                for s in range(STEPS):
                    fill = []
                    if p1 and XC_AT <= s < XC_AT + NG:
                        fill = [(centre, GRP * (s - XC_AT) + k) for k in range(GRP)]
                    if p1 and U_AT <= s < U_AT + NG:
                        fill = [(scale, GRP * (s - U_AT) + k) for k in range(GRP)]
                    if tl and s in (1, 2):
                        fill = [(l_mult, 4 * (s - 1) + k) for k in range(4)]
                    for f, a in fill[0:1]:
                        f(a)
                    if p2 and s < NCH:
                        dve.wait_ge(d_done, NCH * b + s + 1)
                        dve.wait_ge(s_done, NCH * b + s + 1)
                        xc = chunk(xs[par], s)
                        nc.vector.scalar_tensor_tensor(out=xc, in0=pd[:], scalar=vecs[:, 3:4], in1=xc,
                                                       op0=ALU.add, op1=ALU.add).then_inc(x1_done, 1)
                    for f, a in fill[1:]:
                        f(a)
                    if p2 and s >= 1:
                        dve.wait_ge(e_done, NCH * b + s)
                        j = chunk_of(s - 1)
                        nc.vector.tensor_copy(lg[par][:, SUB * j:SUB * (j + 1)], lgp).then_inc(lcopy_done, 1)
                    if tl and s == 0:
                        dve.wait_ge(msq_done, t + 1)
                        tail(nc.vector.scalar_tensor_tensor(out=v2[:], in0=st2[:, SUB:2 * SUB], scalar=EPS, in1=ta[:],
                                                            op0=ALU.add, op1=ALU.subtract))
                        nc.vector.tensor_scalar(v2[:], v2[:], EPS, None, ALU.max).then_inc(var2_ready, 1)
                        dve.wait_ge(y2_ready, t + 1)
                        newton(tail, v2[:], y2[:], tb[:], 0.0)
                        tail(nc.vector.scalar_tensor_tensor(out=tb[:], in0=tb[:], scalar=1.5, in1=y2[:], op0=ALU.add, op1=ALU.mult))
                        tail(nc.vector.tensor_copy(hi[:], tb[:]))
                        nc.vector.scalar_tensor_tensor(out=rstd2_s[:], in0=hi[:].bitcast(F32), scalar=second[:], in1=tb[:],
                                                       op0=ALU.mult, op1=ALU.add).then_inc(rstd2_ready, 1)
                    if tl and s == 3:
                        dve.wait_ge(l_done, 8 * (t + 1))
                        hold(dve, spare[:, 0:1])
                        tail(nc.vector.max(cnd[:, 0:K], lg[nxt][:]))
                        hold(dve, spare[:, 0:1])
                        tail(nc.vector.max_index(top_i[:], cnd[:, 0:K], lg[nxt][:]))
                        tail(nc.vector.tensor_scalar(nmax[:], cnd[:, 0:1], -1.0, None, ALU.mult))
                        tail(nc.vector.tensor_scalar(top_hi[:], top_i[:], 0xFFFFFF00, None, ALU.bitwise_and))
                        nc.vector.scalar_tensor_tensor(out=cnd[:, K:2 * K], in0=top_i[:], scalar=rowoff[:], in1=top_hi[:],
                                                       op0=ALU.add, op1=ALU.add).then_inc(top_ready, 1)
                    if tl and not p2 and s == MERGE_AT:
                        token_norm(0, 0, NB - 1)
                    if tl and s == MERGE_AT + 1:
                        dve.wait_ge(mrg_done, t + 1)
                        m4 = mrg_p.rearrange("e (r k) -> e r k", r=4)
                        tail(nc.vector.tensor_copy(cpix[:].rearrange("e (r k) -> e r k", r=4), m4[:, :, K:2 * K]))
                        tail(nc.vector.tensor_copy(csum[:], m4[:, :, 2 * K]))
                        tail(nc.vector.tensor_copy(cval[:].rearrange("e (r k) -> e r k", r=4), m4[:, :, 0:K]))
                        hold(dve, spare[:, 0:1])
                        tail(nc.vector.max(fval[:], cval[:]))
                        hold(dve, spare[:, 0:1])
                        tail(nc.vector.max_index(fpos[:], fval[:], cval[:]))
                        tail(nc.vector.tensor_tensor(gbm[:, 0:1], fval[:, 0:1], gate_bias[:], ALU.add))
                        nc.vector.tensor_tensor(gbm[:, 1:2], gate_bias[:], gbm[:, 0:1], ALU.subtract).then_inc(bias_ready, 1)
                        tail(nc.vector.tensor_copy(fposf[:], fpos[:]))
                        tail(nc.vector.tensor_tensor(onehot[:], iota32[:].unsqueeze(1).broadcast_to([NE, K, 32]),
                                                     fposf[:].unsqueeze(2).broadcast_to([NE, K, 32]), ALU.is_equal))
                        tail(nc.vector.tensor_tensor(onehot[:], onehot[:], cpix[:].unsqueeze(1).broadcast_to([NE, K, 32]), ALU.mult))
                        tail(nc.vector.tensor_reduce(pv[:, 0:K], onehot[:], AX.X, ALU.add))
                    if tl and s == MERGE_AT + 2:
                        dve.wait_ge(tval_done, 2 * (t + 1))
                        tail(nc.vector.tensor_tensor_reduce(djunk[:], dexp[:], csum[:], 1.0, 0.0, ALU.mult, ALU.add, gbm[:, 2:3]))
                        tail(nc.vector.reciprocal(gbm[:, 3:4], gbm[:, 2:3]))
                        nc.vector.tensor_scalar(pv[:, K:2 * K], tval[:], gbm[:, 3:4], None, ALU.mult).then_inc(pv_ready, 1)
                    if tl and s == MERGE_AT + 3:
                        dve.wait_ge(rep_done, t + 1)
                        tail(nc.vector.tensor_tensor(pvm[:], kmask[:].unsqueeze(1).broadcast_to([P, 2 * GATHERS, 4]),
                                                     rep_p.rearrange("p (a k) -> p a k", k=4), ALU.mult))
                        tail(nc.vector.tensor_reduce(pvt[:], pvm[:], AX.X, ALU.add))
                        tail(nc.vector.tensor_scalar(idxf[:], pvt[:, 0:GATHERS], offs[:], None, ALU.add))
                        at = slice(t, t + 1) if isinstance(t, int) else bass.ds(t, 1)
                        tail(nc.vector.tensor_copy(idx_all[:, at, :], idxf[:].unsqueeze(1)))
                        tail(nc.vector.tensor_copy(px_all[:, at, :], pvt[:, 0:GATHERS].unsqueeze(1)))
                        tail(nc.vector.tensor_copy(tv_all[:, at, :], pvt[:, GATHERS:].unsqueeze(1)))
                        nc.vector.tensor_scalar(offs[:], offs[:], float(PIX), None, ALU.add).then_inc(idx_ready, 1)
                    if tl and s == STEPS - 1:
                        assert tail.n == TAIL_STEPS, tail.n
                    if p1 and s == MEAN_AT:
                        link = Steps(dve, mean_steps, MEAN_STEPS * n)
                        dve.wait_ge(sumx_done, n + 1)
                        link(nc.vector.tensor_copy(hi[:], st1[:, 0:SUB]))
                        nc.vector.scalar_tensor_tensor(out=mean_s[:], in0=hi[:].bitcast(F32), scalar=second[:], in1=st1[:, 0:SUB],
                                                       op0=ALU.mult, op1=ALU.add).then_inc(mean_ready, 1)
                    if p1 and s == RSTD_AT:
                        link = Steps(dve, rstd_steps, RSTD_STEPS * n)
                        dve.wait_ge(y0_ready, n + 1)
                        newton(link, st1[:, SUB:2 * SUB], y0[:], tb[:], EPS_C)
                        link(nc.vector.scalar_tensor_tensor(out=tb[:], in0=tb[:], scalar=1.5, in1=y0[:], op0=ALU.add, op1=ALU.mult))
                        link(nc.vector.tensor_copy(hi[:], tb[:]))
                        nc.vector.scalar_tensor_tensor(out=rstd_s[:], in0=hi[:].bitcast(F32), scalar=second[:], in1=tb[:],
                                                       op0=ALU.mult, op1=ALU.add).then_inc(rstd_ready, 1)
                    if p1 and s == GN_AT:
                        link = Steps(dve, gn_steps, GN_STEPS * n)
                        dve.wait_ge(u_done, NCH * (n + 1))
                        dve.wait_ge(usq_done, NCH * (n + 1))
                        nc.vector.tensor_reduce(gs[:, 0:1], gsum[:], AX.X, ALU.add).then_inc(gnred_ready, 1)
                        nc.vector.tensor_reduce(gs[:, 1:2], gsq[:], AX.X, ALU.add).then_inc(gnred_ready, 1)
                    if p1 and s == GN_AT + 1:
                        dve.wait_ge(gnps_done, 2 * n + 1)
                        link(nc.vector.tensor_copy(gt[:, 0:2], gn_p))
                        link(nc.vector.scalar_tensor_tensor(out=gt[:, 2:3], in0=gt[:, 0:1], scalar=gt[:, 0:1], in1=gt[:, 1:2],
                                                            op0=ALU.mult, op1=ALU.subtract))
                        link(nc.vector.tensor_scalar(gt[:, 2:3], gt[:, 2:3], -1.0, EPS, ALU.mult, ALU.add))
                        link(nc.vector.tensor_scalar(gt[:, 3:4], gt[:, 2:3], EPS, None, ALU.max))
                        nc.vector.tensor_copy(gt[:, 9:10], gt[:, 3:4]).then_inc(gnv_ready, 1)
                        dve.wait_ge(gny_ready, n + 1)
                        newton(link, gt[:, 3:4], gt[:, 4:5], gt[:, 5:6], 0.0)
                        link(nc.vector.scalar_tensor_tensor(out=gt[:, 5:6], in0=gt[:, 5:6], scalar=1.5, in1=gt[:, 4:5],
                                                            op0=ALU.add, op1=ALU.mult))
                        link(nc.vector.tensor_tensor(gt[:, 6:7], vecs[:, 0:1], gt[:, 5:6], ALU.mult))
                        nc.vector.scalar_tensor_tensor(out=gt[:, 7:8], in0=gt[:, 0:1], scalar=gt[:, 6:7], in1=vecs[:, 1:2],
                                                       op0=ALU.mult, op1=ALU.subtract).then_inc(gnbias_ready, 1)
                    if p1 and s == STEPS - 1:
                        wait(dve, c_done, NCH * n)
                        nc.vector.tensor_scalar(w1n[:], w1bd[:], gt[:, 6:7], None, ALU.mult).then_inc(w1n_ready, 1)
                        wait(dve, h_done, NCH * n)
                        dve.wait_ge(gnps_done, 2 * n + 2)
                        nc.vector.tensor_tensor(b1n[:], vecs[:, 2:3], gnb_p, ALU.subtract).then_inc(w1n_ready, 1)
                        for _ in range(GN_STEPS - link.n):
                            link(nc.vector.tensor_copy(gt[:, 11:12], gt[:, 6:7]))

            lns = Steps(dve, ln_steps, 0)

            def token_norm(part, b0, b1):
                dve.wait_ge(rows_in[part], 16 * GATHERS * (b1 - b0))
                n0, n1 = GATHERS * b0, GATHERS * b1
                shape = [P, n1 - n0, C]
                r = rows_all.rearrange("p b g c -> p (b g) c")[:, n0:n1]
                zz = zs.rearrange("p b g c -> p (b g) c")[:, n0:n1]
                q = us[1][:, n0 * C:n1 * C].rearrange("p (n c) -> p n c", c=C)
                mean, var, y, a, rs, ws = (tr[:, i, n0:n1] for i in range(6))
                lns(nc.vector.tensor_reduce(mean, r, AX.X, ALU.add))
                lns(nc.vector.tensor_scalar(mean, mean, 1.0 / C, None, ALU.mult))
                lns(nc.vector.tensor_tensor(zz, r, mean.unsqueeze(2).broadcast_to(shape), ALU.subtract))
                lns(nc.vector.tensor_tensor(q, zz, zz, ALU.mult))
                lns(nc.vector.tensor_reduce(var, q, AX.X, ALU.add))
                nc.vector.tensor_scalar(var, var, 1.0 / C, EPS, ALU.mult, ALU.add).then_inc(rvar_ready, 1)
                dve.wait_ge(ry_ready, part + 1)
                newton(lns, var, y, a, 0.0)
                lns(nc.vector.scalar_tensor_tensor(out=rs, in0=a, scalar=1.5, in1=y, op0=ALU.add, op1=ALU.mult))
                lns(nc.vector.tensor_tensor(ws, rs, tv_all[:, b0:b1].rearrange("p b g -> p (b g)"), ALU.mult))
                nc.vector.tensor_tensor(zz, zz, ws.unsqueeze(2).broadcast_to(shape), ALU.mult).then_inc(z_ready, 1)

            cv = Steps(dve, const_steps, 0)
            nc.vector.memset(w1bd[:], 0.0)
            nc.vector.memset(w2bd[:], 0.0)
            cv(nc.vector.memset(gbd[:], 0.0))
            nc.vector.memset(gt[:, 0:10], 0.0).then_inc(const_d, 1)
            for r in range(4):
                nc.vector.memset(rowoff[32 * r:32 * r + 32, :], float(SUB * (r // 2) + HW * (r % 2)))
            nc.vector.memset(offs[:], 0.0)
            nc.vector.memset(gt[:, 10:11], EPS_C)
            nc.vector.memset(pooled[:], 1.0)
            cv(nc.vector.memset(stat_w[:], 0.0))
            sw = stat_w[:].rearrange("p q m -> p (q m)")
            for h in range(HALVES):
                for d in range(2):
                    ins = nc.vector.memset(sw[C * h:C * h + C, h + 16 * d:h + 16 * d + 34 * 7 + 1:34], 1.0 / C)
            cv(ins)
            dve.wait_ge(const_p, CONST_P)
            nc.vector.tensor_copy(spread[:], lg[0][:, 0:1024])
            nc.vector.tensor_copy(rep[:].rearrange("e (k f) -> e k f", k=4),
                                  ident[0:NE, 0:NE].unsqueeze(1).broadcast_to([NE, 4, NE]))
            nc.vector.tensor_reduce(kmask[:], ident[:].rearrange("p (k e) -> p k e", k=4), AX.X, ALU.add)
            cv(nc.vector.tensor_reduce(esel[:], ident[:].rearrange("p (k e) -> p e k", k=4), AX.X, ALU.add))
            cv(nc.vector.memset(cen[:], 0.0))
            for h in range(HALVES):
                ins = nc.vector.memset(cen[C * h:C * h + C, C * h:C * h + C], 1.0 / C)
            cv(ins)
            nc.vector.tensor_tensor(cen[:], ident[:], cen[:], ALU.subtract).then_inc(const_v, 1)
            dve.wait_ge(w_in, 16 * 15)
            dve.wait_ge(const_t, 1)
            nc.vector.tensor_copy(gcen[:], pe_b[:, 0:C]).then_inc(const_v, 1)
            dve.wait_ge(const_v, CONST_V + 1)

            iteration(-1, 1, True, False, False)
            iteration(0, 0, True, True, False)
            with dve.Fori(0, 3) as i:
                iteration(2 * i + 1, 1, True, True, True)
                iteration(2 * i + 2, 0, True, True, True)
            iteration(7, 1, False, True, True)
            iteration(8, 0, False, False, True)

            token_norm(1, NB - 1, NB)
            dve.wait_ge(pool_done, 1)
            nc.vector.tensor_copy(pooled[0:C, :, :].rearrange("c e b -> c b e"),
                                  bc[0][0:C, 0:NE * NB].rearrange("c (b e) -> c b e", b=NB)).then_inc(pooled_ready, 1)

            dve.wait_ge(pex_done, 1)
            nc.vector.tensor_copy(tb[0:C, 0:NE], pt[0:C, 0:NE]).then_inc(ebias_ready, 1)
            dve.wait_ge(ebias_ready, 1)
            dve.wait_ge(l2_done, 1)
            for kk in range(4):
                ins = nc.vector.tensor_tensor(
                    us[1][0:C, 0:NB * P].rearrange("o (b k e) -> o k e b", b=NB, k=4)[:, kk],
                    tb[0:C, 0:NE].unsqueeze(2).broadcast_to([C, NE, NB]),
                    pd[0:C, 0:NE * NB].rearrange("o (e b) -> o e b", b=NB), ALU.add)
            ins.then_inc(eo_ready, 1)
            dve.wait_ge(eo_ready, 1)
            dve.wait_ge(usq_done, NCH * NB)
            ins = nc.vector.memset(ones, 1.0)
            for b in range(NB):
                dve.wait_ge(ob_done, b + 1)
                if b >= 1:
                    dve.wait_ge(add_done, b)
                for g in range(GATHERS):
                    nc.vector.tensor_scalar(hid[0][:, P * g:P * g + P], ident[:], px_all[:, b, g:g + 1], None, ALU.mult)
                    ins = nc.vector.tensor_scalar(z[:, g, :], pt[:, 0:C], tv_all[:, b, g:g + 1], None, ALU.mult)
                ins.then_inc(diag_ready, 1)
                dve.wait_ge(pxr_done, b + 1)
                for g in range(GATHERS):
                    ins = nc.vector.tensor_scalar(sqc[:, g, 0:GATHERS * P], bc[0][:, 0:GATHERS * P], px_all[:, b, g:g + 1],
                                                  None, ALU.is_equal)
                ins.then_inc(eq_ready, 1)
                dve.wait_ge(add_done, b + 1)
                rv = rows_all[:, b].rearrange("p g c -> p (g c)")
                nc.vector.tensor_tensor(rv, rv, bc[1][:, 0:GATHERS * C], ALU.add).then_inc(row_ready, 1)

        @block.gpsimd
        def _(pool):
            cp = Steps(pool, pool_steps, 0)
            nc.gpsimd.memset(ident[:], 0.0)
            nc.gpsimd.memset(gsel[:], 1.0 / (GN_GROUP * PIX))
            nc.gpsimd.memset(lg[0][:, 0:1024], 0.0)
            nc.gpsimd.memset(second[:], -1.0)
            nc.gpsimd.iota(iota32[:], pattern=[[1, 32]], base=0, channel_multiplier=0, allow_small_or_imprecise_dtypes=True)
            cp(nc.gpsimd.memset(lg[1][:, 0:1], 0.0))
            cp(nc.gpsimd.affine_select(out=ident[:], in_=ident[:], compare_op=ALU.not_equal, fill=1.0, base=0,
                                       pattern=[[-1, P]], channel_multiplier=1))
            for q in range(4):
                for copy in range(2):
                    v = lg[0][32 * q:32 * q + 32, 0:1024].rearrange("p (r y) -> p r y", r=16)
                    cp(nc.gpsimd.affine_select(out=v, in_=v, compare_op=ALU.not_equal, fill=1.0, base=-16 * copy,
                                               pattern=[[-1, 16], [0, C]], channel_multiplier=1))
                v = second[32 * q:32 * q + 32, :]
                cp(nc.gpsimd.affine_select(out=v, in_=v, compare_op=ALU.is_ge, fill=0.0, base=-16,
                                           pattern=[[0, 1]], channel_multiplier=1))
            for h in range(HALVES):
                v = gsel[C * h:C * h + C, :].rearrange("p (a g i) -> p a g i", a=2, g=C // GN_GROUP)
                pat = [[0, 2], [-GN_GROUP, C // GN_GROUP], [0, GN_GROUP]]
                cp(nc.gpsimd.affine_select(out=v, in_=v, compare_op=ALU.is_ge, fill=0.0, base=0, pattern=pat,
                                           channel_multiplier=1))
                pat = [[0, 2], [GN_GROUP, C // GN_GROUP], [0, GN_GROUP]]
                cp(nc.gpsimd.affine_select(out=v, in_=v, compare_op=ALU.is_ge, fill=0.0, base=GN_GROUP - 1, pattern=pat,
                                           channel_multiplier=-1))
            nc.gpsimd.memset(lg[1][:, 0:1], 0.0).then_inc(const_p, 1)

            def iteration(it, par, p1, p2, tl):
                b, n, t = it, it + 1, it - 1
                nxt = 1 - par
                for s in range(STEPS):
                    if p2 and s < NCH:
                        pool.wait_ge(x1_done, NCH * b + s + 1)
                        wait(pool, grp_done, NG * b + s // GRP)
                        xc = chunk(xs[par], s)
                        nc.gpsimd.tensor_tensor(sqx[:, s % GRP, :], xc, xc, ALU.mult).then_inc(sqx_done, 1)
                    if p1 and U_AT <= s < U_AT + NG:
                        for k in range(GRP * (s - U_AT), GRP * (s - U_AT + 1)):
                            pool.wait_ge(u_done, NCH * n + k + 1)
                            nc.gpsimd.tensor_tensor(chunk(xs[nxt], k), chunk(xs[nxt], k), chunk(us[nxt], k),
                                                    ALU.add).then_inc(s_done, 1)
            iteration(-1, 1, True, False, False)
            iteration(0, 0, True, True, False)
            with pool.Fori(0, 3) as i:
                iteration(2 * i + 1, 1, True, True, True)
                iteration(2 * i + 2, 0, True, True, True)
            iteration(7, 1, False, True, True)
            iteration(8, 0, False, False, True)
            for q in range(2):
                pool.wait_ge(stored[q], 16 * (NCH // 2) * NB)
            pool.wait_ge(grp_done, NG * NB)
            for b in range(NB):
                if b in (0, NB - 1):
                    pool.wait_ge(idx_ready, NB - 1 if b == 0 else NB)
                for g in range(GATHERS):
                    nc.gpsimd.indirect_dma_start(
                        rows_all[:, b, g, :], None, out_rows,
                        bass.IndirectOffsetOnAxis(ap=idx_all[:, b, g:g + 1], axis=0)).then_inc(rows_in[b == NB - 1], 16)
            for b in range(NB):
                pool.wait_ge(row_ready, b + 1)
                for g in range(GATHERS):
                    wait(pool, scattered, 16 * (GATHERS * b + g))
                    nc.gpsimd.indirect_dma_start(
                        out_rows, bass.IndirectOffsetOnAxis(ap=idx_all[:, b, g:g + 1], axis=0),
                        rows_all[:, b, g, :], None).then_inc(scattered, 16)
            pool.wait_ge(scattered, 16 * GATHERS * NB)


def kernel(x, L0_conv_gn_w, L0_conv_gn_b, L0_conv_w1, L0_conv_b1, L0_conv_w2, L0_conv_b2,
           L0_ffn_gate_w, L0_ffn_gate_b, L0_ffn_weight1, L0_ffn_weight2):
    import numpy as np
    import concourse.bacc as bacc
    from concourse.bass_utils import run_bass_kernel_spmd

    ins = {
        "x": np.ascontiguousarray(x).reshape(NB, C, PIX),
        "gn_w": L0_conv_gn_w, "gn_b": L0_conv_gn_b,
        "w1T": np.asarray(L0_conv_w1).T, "b1": L0_conv_b1,
        "w2T": np.asarray(L0_conv_w2).T, "b2": L0_conv_b2,
        "gateT": np.asarray(L0_ffn_gate_w).T, "gate_b": L0_ffn_gate_b,
        "e_w1": L0_ffn_weight1, "e_w2": L0_ffn_weight2,
    }
    nc = bacc.Bacc("TRN2", target_bir_lowering=False, num_devices=1)
    arrays, args = {}, []
    for name, a in ins.items():
        a = np.ascontiguousarray(a)
        arrays[f"in_{name}"] = a
        args.append(nc.dram_tensor(f"in_{name}", a.shape, mybir.dt.from_np(a.dtype), kind="ExternalInput").ap())
    args.append(nc.dram_tensor("out_rows", (NB, PIX, C), F32, kind="ExternalOutput").ap())
    mk_metaformer_kernel(nc, *args)
    r = run_bass_kernel_spmd(nc, [arrays], core_ids=[0])
    got = r.results[0]["out_rows"]
    return np.ascontiguousarray(got.transpose(0, 2, 1)).reshape(NB, C, 128, 128)
```

```python
from contextlib import ExitStack

import concourse.bass as bass
from concourse import mybir

F32 = mybir.dt.float32
F32R = mybir.dt.float32r
U32 = mybir.dt.uint32
ALU = mybir.AluOpType
ACT = mybir.ActivationFunctionType
AX = mybir.AxisListType

P = 128
C = 64
HALVES = 2
NB = 8
PIX = 128 * 128
HW = PIX // HALVES
CH = 512
SUB = 256
NCH = HW // CH
GRP = 4
NG = NCH // GRP
NE = 32
K = 8
HID = 256
EPS_C = 1e-6
EPS = 1e-5
GN_GROUP = 8
GATHERS = K * NE // P
PIECES = 4
PIECE = HW // 2 // PIECES
CAND = PIECES * K
MRG = 2 * CAND + PIECES

STEPS = NCH + 1
L_AT = {1: (0, 1), 2: (2, 3), 3: (4, 5), 8: (6, 7)}
C_AT = {s: tuple(range(GRP * (s - 4), GRP * (s - 3))) for s in range(4, 8)}
S_AT = {9: (0, 1), 10: (2, 3, 4, 5), 11: (6, 7, 8, 9), 12: (10, 11, 12, 13), 13: (14, 15)}
ADD_AT = {10: (0, 1), 11: (2, 3), 12: (4, 5), 13: (6, 7), 14: (8, 9), 15: (10, 11, 12), 16: (13, 14, 15)}
MAX_AT, FIND_AT, EXP_AT = {1: 0, 2: 1, 3: 2, 9: 3}, {1: 0, 2: 1, 4: 2, 9: 3}, {2: 0, 3: 1, 8: 2, 10: 3}
SUMX_AT = {0: (0, 1), 1: (2,), 3: (3,)}
MEAN_AT, RSTD_AT, GN_AT, MERGE_AT = 3, 8, 13, 11
NL, NSPREAD = 2 * PIECES, 2 * NCH


def spreads(s, p1, tl):
    def of(t):
        return ([("L", k) for k in L_AT.get(t, ())] if tl else []) + \
               ([("C", k) for k in C_AT.get(t, ())] + [("S", k) for k in S_AT.get(t, ())] if p1 else [])
    return of(s), sum(len(of(t)) for t in range(s))


def spread_base(it):
    if isinstance(it, int):
        return (it + 1) * NSPREAD if it < 1 else 2 * NSPREAD + (NL + NSPREAD) * min(it - 1, 6) + NL * max(it - 7, 0)
    return 2 * NSPREAD + (NL + NSPREAD) * (it - 1)


def chunk_of(s):
    return GRP * (s % GRP) + s // GRP


def spread_end(it, kind, k, p1, tl):
    every = [job for s in range(STEPS) for job in spreads(s, p1, tl)[0]]
    return spread_base(it) + every.index((kind, k)) + 1


def mk_metaformer_kernel(nc, x, gn_w, gn_b, w1T, b1, w2T, b2, gateT, gate_b, e_w1, e_w2, out):
    ctx = ExitStack()
    with ctx:
        def sb(name, shape, dt=F32):
            return ctx.enter_context(nc.sbuf_tensor(name, shape, dt))

        def bank(name):
            return ctx.enter_context(nc.psum_tensor(name, [P, CH], F32))

        def sem(name):
            return ctx.enter_context(nc.semaphore(name))

        xs = [sb(f"xs{i}", [P, HW]) for i in range(2)]
        us = [sb(f"us{i}", [P, HW]) for i in range(2)]
        lg = [sb(f"lg{i}", [P, HW // 2]) for i in range(2)]
        hid = [sb(f"hid{i}", [P, CH]) for i in range(2)]
        tok = [sb(f"tok{i}", [P, HALVES, GRP, C]) for i in range(2)]
        sqc = sb("sqc", [P, GRP, CH])
        sqx = sb("sqx", [P, GRP, CH])
        junk = sb("junk", [P, 2, CH], mybir.dt.bfloat16)

        ident = sb("ident", [P, P])
        stat_w = sb("stat_w", [P, 8, 32])
        spread = sb("spread", [P, 16 * 64], F32R)
        second = sb("second", [P, 1])
        gsel = sb("gsel", [P, P])
        w1bd = sb("w1bd", [P, P])
        w1n = [sb(f"w1n{i}", [P, P]) for i in range(2)]
        cen = w1n[1]
        w2bd = sb("w2bd", [P, P])
        gbd = sb("gbd", [P, C])
        gcen = sb("gcen", [P, C])
        vecs = sb("vecs", [P, 4])
        gate_bias = sb("gate_bias", [NE, 1])
        ones = junk[:, 0, 0:2 * P].bitcast(F32)
        kmask = sb("kmask", [P, 4])
        esel = sb("esel", [P, NE])
        rep = sb("rep", [NE, P])
        iota = sb("iota", [NE, 4 * CAND])
        rowoff = sb("rowoff", [P, 1])

        hi = sb("hi", [P, SUB], F32R)
        mean_s = sb("mean_s", [P, SUB], F32R)
        rstd_s = sb("rstd_s", [P, SUB], F32R)
        rstd2_s = sb("rstd2_s", [P, SUB], F32R)
        lnv, y0, ta, tb = (sb(n, [P, SUB]) for n in ("lnv", "y0", "ta", "tb"))
        v2, y2 = lnv, y0
        gsum = sb("gsum", [P, NCH])
        gsq = sb("gsq", [P, NCH])
        gs = sb("gs", [P, 2])
        gt = sb("gt", [P, 12])
        b1n = sb("b1n", [P, 2])
        spare = sb("spare", [P, 2])

        cnd = sb("cnd", [P, MRG])
        top_i = sb("top_i", [P, K], U32)
        top_hi = sb("top_hi", [P, K], U32)
        nmax = sb("nmax", [P, PIECES])
        cval = sb("cval", [NE, 4 * CAND])
        cpix = sb("cpix", [NE, 4 * CAND])
        csum = sb("csum", [NE, 4 * PIECES])
        fval = sb("fval", [NE, K])
        fpos = sb("fpos", [NE, K], U32)
        fposf = sb("fposf", [NE, K])
        onehot = junk[0:NE].rearrange("p a n -> p (a n)").bitcast(F32).rearrange("p (k n) -> p k n", k=K // 2)
        gbm = sb("gbm", [NE, 4])
        tval = sb("tval", [NE, K])
        dexp = sb("dexp", [NE, 4 * PIECES])
        djunk = sb("djunk", [NE, 4 * PIECES])
        pv = sb("pv", [NE, 2 * K])
        pvm = sb("pvm", [P, 2 * GATHERS, 4])
        pvt = sb("pvt", [P, 2 * GATHERS])
        offs = sb("offs", [P, 1])
        idxf = sb("idxf", [P, GATHERS])
        idx_all = sb("idx_all", [P, NB, GATHERS], U32)
        px_all = sb("px_all", [P, NB, GATHERS])
        tv_all = sb("tv_all", [P, NB, GATHERS])
        rows_all = sqx[:].rearrange("p g n -> p (g n)")[:, 0:NB * GATHERS * C].rearrange(
            "p (b g c) -> p b g c", b=NB, g=GATHERS)
        zs = sqc[:].rearrange("p g n -> p (g n)")[:, 2 * CH:4 * CH].rearrange(
            "p (b g c) -> p b g c", b=NB, g=GATHERS)
        tr = sb("tr", [P, 6, NB * GATHERS])
        z = sb("z", [P, GATHERS, C])
        pooled = lg[0][0:C + 1, 0:NE * NB].rearrange("c (e b) -> c e b", b=NB)

        bc = [bank(f"bc{i}") for i in range(2)]
        pc, pd, pe_b, pt = bank("pc"), bank("pd"), bank("pe_b"), bank("pt")
        st1, st2 = bank("st1"), bank("st2")
        lgp = pe_b[:, 0:SUB]
        mrg_p = st1[0:NE, 0:4 * MRG]
        rep_p = st1[:, 300:300 + 2 * K]
        gn_p = st1[:, 340:342]
        gnb_p = st1[:, 344:345]

        w_in, x_in = sem("w_in"), [sem(f"x_in{m}") for m in range(NG)]
        const_p, const_v, const_d, const_t = sem("const_p"), sem("const_v"), sem("const_d"), sem("const_t")
        sumx_done, mean_ready, mean_steps = sem("sumx_done"), sem("mean_ready"), sem("mean_steps")
        bc_filled, bc_used = sem("bc_filled"), sem("bc_used")
        sqc_done, sumsq_done = sem("sqc_done"), sem("sumsq_done")
        lnv_done, y0_ready, rstd_steps, rstd_ready = (sem(n) for n in ("lnv_done", "y0_ready", "rstd_steps", "rstd_ready"))
        usq_done, s_done = sem("usq_done"), sem("s_done")
        gn_steps, gnred_ready, gnps_done, gnv_ready = (sem(n) for n in ("gn_steps", "gnred_ready", "gnps_done", "gnv_ready"))
        gnln_done, gny_ready, gnbias_ready, w1n_ready = (sem(n) for n in ("gnln_done", "gny_ready", "gnbias_ready", "w1n_ready"))
        c_done, h_done, d_done, x1_done = (sem(n) for n in ("c_done", "h_done", "d_done", "x1_done"))
        e_done, lcopy_done, t_done, tok_done = (sem(n) for n in ("e_done", "lcopy_done", "t_done", "tok_done"))
        sqx_done, grp_done = sem("sqx_done"), sem("grp_done")
        stored = [sem(f"stored{i}") for i in range(2)]
        msq_done, var2_ready, ln2_done, y2_ready = (sem(n) for n in ("msq_done", "var2_ready", "ln2_done", "y2_ready"))
        tail_steps, rstd2_ready = sem("tail_steps"), sem("rstd2_ready")
        top_ready, expl_done, mrg_done, bias_ready = (sem(n) for n in ("top_ready", "expl_done", "mrg_done", "bias_ready"))
        tval_done, pv_ready, rep_done, idx_ready = (sem(n) for n in ("tval_done", "pv_ready", "rep_done", "idx_ready"))
        rows_in = [sem("rows_in0"), sem("rows_in1")]
        ln_steps, rvar_ready, rln_done, ry_ready = (sem(n) for n in ("ln_steps", "rvar_ready", "rln_done", "ry_ready"))
        z_ready, pool_done, pooled_ready = (sem(n) for n in ("z_ready", "pool_done", "pooled_ready"))
        ew_in, l1_done, gelu_done, l2_done = (sem(n) for n in ("ew_in", "l1_done", "gelu_done", "l2_done"))
        eo_ready, ob_done, diag_ready = (sem(n) for n in ("eo_ready", "ob_done", "diag_ready"))
        pxr_done, eq_ready, add_done, row_ready, scattered = (
            sem(n) for n in ("pxr_done", "eq_ready", "add_done", "row_ready", "scattered"))
        pex_done, ebias_ready = sem("pex_done"), sem("ebias_ready")
        pool_steps, const_steps = sem("pool_steps"), sem("const_steps")

        x_h = x.rearrange("b c (h m q n) -> b h c m q n", h=HALVES, m=GRP, q=NG)
        out_t = out.rearrange("b (h j p t) c -> b j p h (t c)", h=HALVES, j=NCH, p=P)
        out_rows = out.rearrange("b p c -> (b p) c")

        MEAN_STEPS, RSTD_STEPS, GN_STEPS, TAIL_STEPS = 1, 4, 7, 46
        CONST_P, CONST_V = 1, 1

        def chunk(buf, s):
            j = chunk_of(s)
            return buf[:, CH * j:CH * (j + 1)]

        def piece(buf, i):
            return buf[:, PIECE * i:PIECE * (i + 1)]

        def wait(eng, s, value):
            if not isinstance(value, int) or value > 0:
                eng.wait_ge(s, value)

        def hold(eng, cell):
            eng.tensor_tensor(cell, second[:, 0:1], second[:, 0:1], ALU.mult)

        class Steps:
            def __init__(self, eng, s, base):
                self.eng, self.sem, self.base, self.n = eng, s, base, 0

            def __call__(self, ins):
                self.n += 1
                ins.then_inc(self.sem, 1)
                self.eng.wait_ge(self.sem, self.base + self.n)

        def newton(link, v, y, a, eps):
            link(nc.vector.scalar_tensor_tensor(out=a, in0=v, scalar=eps, in1=y, op0=ALU.add, op1=ALU.mult))
            link(nc.vector.scalar_tensor_tensor(out=a, in0=a, scalar=-0.5, in1=y, op0=ALU.mult, op1=ALU.mult))

        block = ctx.enter_context(nc.Block())

        @block.sync
        def _(sp):
            def load(b, m, slot):
                for h in range(HALVES):
                    dst = xs[slot][C * h:C * h + C, :].rearrange("c (k q n) -> c k q n", k=GRP, q=NG)[:, :, m, :]
                    src = x_h[b, h, :, :, m, :] if isinstance(b, int) else \
                        x_h[bass.ds(b, 1), h, :, :, m, :].rearrange("a c m n -> (a c) m n")
                    sp.dma_start(dst, src).then_inc(x_in[m], 16)

            for m in range(NG):
                load(0, m, 0)
            for vec, src in enumerate((gn_w, gn_b, b1, b2)):
                for h in range(HALVES):
                    sp.dma_start(vecs[C * h:C * h + C, vec:vec + 1], src.rearrange("(c a) -> c a", a=1)).then_inc(w_in, 16)
            sp.dma_start(gate_bias[:], gate_b.rearrange("(e a) -> e a", a=1)).then_inc(w_in, 16)
            sp.wait_ge(const_d, 1)
            for h in range(HALVES):
                r = slice(C * h, C * h + C)
                sp.dma_start(w1bd[r, r], w1T).then_inc(w_in, 16)
                sp.dma_start(w2bd[r, r], w2T).then_inc(w_in, 16)
                sp.dma_start(gbd[r, NE * h:NE * h + NE], gateT).then_inc(w_in, 16)
            for m in range(NG):
                load(1, m, 1)

            def iteration(it, par, loads):
                for s in range(NCH + 1):
                    if s < NCH:
                        sp.wait_ge(tok_done, it * NCH + s + 1)
                        dst = out_t[it, chunk_of(s)] if isinstance(it, int) else \
                            out_t[bass.ds(it, 1), chunk_of(s)].rearrange("a p h n -> (a p) h n")
                        sp.dma_start(dst, tok[s % 2][:].rearrange("p h t c -> p h (t c)")).then_inc(stored[s % 2], 16)
                    if loads and (s > GRP and s % GRP == 1 or s == NCH):
                        m = NG - 1 if s == NCH else s // GRP - 1
                        sp.wait_ge(grp_done, it * NG + m + 1)
                        load(it + 2, m, par)

            iteration(0, 0, True)
            with sp.Fori(0, 2) as i:
                iteration(2 * i + 1, 1, True)
                iteration(2 * i + 2, 0, True)
            iteration(5, 1, True)
            iteration(6, 0, False)
            sp.wait_ge(grp_done, 7 * NG)
            sp.dma_start(us[0][0:C + 1, :].rearrange("d (e n) -> d e n", e=NE),
                         e_w1.rearrange("e d n -> d e n")).then_inc(ew_in, 16)
            for k in range(2):
                sp.dma_start(xs[0][:, 0:NE * 2 * C].rearrange("p (e k o) -> p e k o", e=NE, k=2)[:, :, k, :],
                             e_w2[:, k * P:(k + 1) * P, :].rearrange("e p o -> p e o")).then_inc(ew_in, 16)
            sp.dma_start(xs[0][0:NE, NE * 2 * C:NE * 2 * C + C], e_w2[:, HID, :]).then_inc(ew_in, 16)
            iteration(7, 1, False)

        @block.tensor
        def _(pe):
            def sub_sum(dst, src, s, sub, start):
                c, q = s % GRP, 2 * (s // GRP) + sub
                col = CH * chunk_of(s) if src.shape[-1] == HW else CH * (s % GRP)
                return pe.matmul(dst[32 * c:32 * c + 32], stat_w[:, q, :], src[:, col + SUB * sub:col + SUB * sub + SUB],
                                 start=start, stop=True, skip_group_check=True)

            def sum_group(dst, src, m, first):
                for sub in range(2):
                    for c in range(GRP):
                        mm = sub_sum(dst, src, GRP * m + c, sub, first and m == 0 and sub == 0)
                return mm

            def spread_chunk(dst, stat, j):
                c = j // GRP
                for sub in range(2):
                    w = 2 * C * (2 * (j % GRP) + sub)
                    mm = pe.matmul(dst[:, SUB * sub:SUB * sub + SUB], spread[32 * c:32 * c + 32, w:w + 2 * C],
                                   stat[32 * c:32 * c + 32, :], start=True, stop=True)
                return mm

            def iteration(it, par, p1, p2, tl):
                b, n, t = it, it + 1, it - 1
                nxt = 1 - par

                def spread_stat(job, i, s):
                    kind, k = job
                    count = spread_base(it) + i
                    if kind == "L" and k == 0:
                        pe.wait_ge(rstd2_ready, t + 1)
                    if kind == "C" and k == 0:
                        pe.wait_ge(mean_ready, n + 1)
                    if kind == "S" and k == 0:
                        pe.wait_ge(rstd_ready, n + 1)
                    wait(pe, bc_used, count - 1)
                    if kind == "L":
                        for h in range(2):
                            j = 2 * k + h
                            c, w = j // GRP, 4 * C * (j % GRP)
                            mm = pe.matmul(bc[i % 2][:, SUB * h:SUB * h + SUB], spread[32 * c:32 * c + 32, w:w + 4 * C:2],
                                           rstd2_s[32 * c:32 * c + 32, :], start=True, stop=True)
                    else:
                        mm = spread_chunk(bc[i % 2], mean_s if kind == "C" else rstd_s, chunk_of(k))
                    mm.then_inc(bc_filled, 1)

                def conv1(b, par, s):
                    if s == 0:
                        pe.wait_ge(w1n_ready, 2 * (b + 1))
                    wait(pe, h_done, NCH * b + s)
                    pe.matmul(pc[:], w1n[par][:], chunk(us[par], s), start=True, stop=True).then_inc(c_done, 1)

                def conv2(s):
                    pe.wait_ge(h_done, NCH * b + s + 1)
                    wait(pe, x1_done, NCH * b + s)
                    pe.matmul(pd[:], w2bd[:], hid[s % 2][:], start=True, stop=True).then_inc(d_done, 1)

                def logits_and_tokens(s):
                    pe.wait_ge(x1_done, NCH * b + s + 1)
                    wait(pe, lcopy_done, NCH * b + s)
                    col = CH * chunk_of(s)
                    for slot in range(2):
                        mm = pe.matmul(lgp[C * slot:C * slot + C], gcen[:],
                                       xs[par][:, col + SUB * slot:col + SUB * slot + SUB], start=True, stop=True)
                    mm.then_inc(e_done, 1)
                    wait(pe, tok_done, NCH * b + s)
                    for k in range(4):
                        mm = pe.transpose(pt[:, P * k:P * k + P], xs[par][:, col + k:col + CH:4], ident[:])
                    mm.then_inc(t_done, 1)

                for s in range(STEPS):
                    jobs, before = spreads(s, p1, tl)
                    jobs = [(job, before + i, s) for i, job in enumerate(jobs)]
                    if p2 and s + 1 < NCH:
                        conv1(b, par, s + 1)
                    if p1 and s == NCH:
                        conv1(n, nxt, 0)
                    for job in jobs[:len(jobs) // 2]:
                        spread_stat(*job)
                    if p2 and s < NCH:
                        conv2(s)
                    for job in jobs[len(jobs) // 2:]:
                        spread_stat(*job)
                    if p1 and s - 1 in C_AT:
                        m = s - 1 - min(C_AT)
                        pe.wait_ge(sqc_done, NCH * n + GRP * (m + 1))
                        sum_group(st1[:, SUB:2 * SUB], sqc[:].rearrange("p g n -> p (g n)"), m, True).then_inc(sumsq_done, 1)
                    if p2 and s >= 1:
                        logits_and_tokens(s - 1)
                    if p2 and s >= GRP and s % GRP == 0:
                        if s == GRP and tl:
                            pe.wait_ge(var2_ready, t + 1)
                        sum_group(st2[:, 0:SUB], xs[par][:], s // GRP - 1, True)
                    if p2 and (s > GRP and s % GRP == 1 or s == NCH):
                        m = NG - 1 if s == NCH else s // GRP - 1
                        pe.wait_ge(sqx_done, NCH * b + GRP * (m + 1))
                        sum_group(st2[:, SUB:2 * SUB], sqx[:].rearrange("p g n -> p (g n)"), m, False).then_inc(grp_done, 1)
                    if p1 and s in SUMX_AT:
                        if s == 0:
                            wait(pe, w1n_ready, 2 * n)
                            if tl and (not isinstance(it, int) or it > 1):
                                wait(pe, idx_ready, t)
                        for m in SUMX_AT[s]:
                            pe.wait_ge(x_in[m], 32 * (n + 1))
                            mm = sum_group(st1[:, 0:SUB], xs[nxt][:], m, True)
                        if m == NG - 1:
                            mm.then_inc(sumx_done, 1)
                    if tl and s == MERGE_AT:
                        pe.wait_ge(top_ready, PIECES * (t + 1))
                        pe.wait_ge(expl_done, PIECES * (t + 1))
                        if p1:
                            pe.wait_ge(rstd_ready, n + 1)
                        for r in range(4):
                            mm = pe.matmul(mrg_p[:, MRG * r:MRG * r + MRG], ident[:, NE * r:NE * r + NE], cnd[:],
                                           start=True, stop=True)
                        mm.then_inc(mrg_done, 1)
                    if p1 and s == GN_AT + 1:
                        pe.wait_ge(gnred_ready, 2 * (n + 1))
                        pe.matmul(gn_p, gsel[:], gs[:], start=True, stop=True).then_inc(gnps_done, 1)
                    if p1 and s == GN_AT + 2:
                        pe.wait_ge(gnbias_ready, n + 1)
                        pe.matmul(gnb_p, w1bd[:], gt[:, 7:8], start=True, stop=True).then_inc(gnps_done, 1)
                    if tl and s == STEPS - 1:
                        pe.wait_ge(pv_ready, t + 1)
                        pe.matmul(rep_p, rep[:], pv[:], start=True, stop=True).then_inc(rep_done, 1)

            pe.wait_ge(const_v, CONST_V)
            pe.wait_ge(w_in, 16 * 15)
            pe.matmul(pe_b[:, 0:C], cen[:], gbd[:], start=True, stop=True).then_inc(const_t, 1)
            pe.wait_ge(const_v, CONST_V + 1)
            iteration(-1, 1, True, False, False)
            iteration(0, 0, True, True, False)
            with pe.Fori(0, 3) as i:
                iteration(2 * i + 1, 1, True, True, True)
                iteration(2 * i + 2, 0, True, True, True)
            iteration(7, 1, False, True, True)
            iteration(8, 0, False, False, True)

            ew1 = us[0][0:C + 1, :].rearrange("d (e n) -> d e n", e=NE)
            ew2 = xs[0][:, 0:NE * 2 * C].rearrange("p (e k o) -> p e k o", e=NE, k=2)
            eb2 = xs[0][0:NE, NE * 2 * C:NE * 2 * C + C]
            pe.wait_ge(ew_in, 64)
            pe.transpose(pt[0:C, 0:NE], eb2, ident[0:NE, 0:NE]).then_inc(pex_done, 1)
            pe.wait_ge(z_ready, 2)
            for b in range(NB):
                for g in range(GATHERS):
                    mm = pe.matmul(bc[0][0:C, NE * b:NE * b + NE], zs[:, b, g, :], esel[:],
                                   start=(g == 0), stop=(g == GATHERS - 1))
            mm.then_inc(pool_done, 1)
            pe.wait_ge(pooled_ready, 1)
            for e in range(NE):
                for k in range(2):
                    mm = pe.matmul(pc[:, 16 * e + 8 * k:16 * e + 8 * k + 8], ew1[:, e, P * k:P * k + P], pooled[:, e, :],
                                   start=True, stop=True)
            mm.then_inc(l1_done, 1)
            pe.wait_ge(gelu_done, 1)
            for e in range(NE):
                for k in range(2):
                    mm = pe.matmul(pd[0:C, 8 * e:8 * e + 8], ew2[:, e, k, :], hid[0][:, 16 * e + 8 * k:16 * e + 8 * k + 8],
                                   start=(k == 0), stop=(k == 1))
            mm.then_inc(l2_done, 1)
            pe.wait_ge(eo_ready, 1)
            for b in range(NB):
                wait(pe, row_ready, b)
                pe.matmul(pt[:, 0:C], us[1][0:C, P * b:P * b + P], ident[0:C, 0:C],
                          start=True, stop=True).then_inc(ob_done, 1)
                pe.wait_ge(diag_ready, b + 1)
                for g in range(GATHERS):
                    mm = pe.matmul(bc[0][:, P * g:P * g + P], ones, hid[0][:, P * g:P * g + P], start=True, stop=True)
                mm.then_inc(pxr_done, 1)
                pe.wait_ge(eq_ready, b + 1)
                for g in range(GATHERS):
                    for f in range(GATHERS):
                        mm = pe.matmul(bc[1][:, C * g:C * g + C], sqc[:, f, P * g:P * g + P], z[:, f, :],
                                       start=(f == 0), stop=(f == GATHERS - 1))
                mm.then_inc(add_done, 1)

        @block.scalar
        def _(act):
            def rsqrt_start(v, ln, y, eps, ln_done, y_ready, count):
                nc.scalar.activation(ln, v, ACT.Ln, bias=eps).then_inc(ln_done, 1)
                act.wait_ge(ln_done, count)
                nc.scalar.activation(y, ln, ACT.Exp, scale=-0.5).then_inc(y_ready, 1)

            def token_rsqrt(part, b0, b1):
                act.wait_ge(rvar_ready, part + 1)
                n = slice(GATHERS * b0, GATHERS * b1)
                rsqrt_start(tr[:, 1, n], tr[:, 3, n], tr[:, 2, n], 0.0, rln_done, ry_ready, part + 1)

            def iteration(it, par, p1, p2, tl):
                b, n, t = it, it + 1, it - 1
                nxt = 1 - par

                def relu(b, par, s):
                    act.wait_ge(c_done, NCH * b + s + 1)
                    wait(act, d_done, NCH * b + s - 1)
                    if s == 0:
                        act.wait_ge(w1n_ready, 2 * (b + 1))
                    nc.scalar.activation(hid[s % 2][:], pc[:], ACT.Relu, bias=b1n[:, par:par + 1]).then_inc(h_done, 1)

                def square_xc(k):
                    act.wait_ge(bc_used, spread_end(it, "C", k, p1, tl))
                    wait(act, sumsq_done, NG * n + k // GRP)
                    nc.scalar.activation(sqc[:, k % GRP, :], chunk(us[nxt], k), ACT.Square).then_inc(sqc_done, 1)

                def square_u(k):
                    act.wait_ge(bc_used, spread_end(it, "S", k, p1, tl))
                    wait(act, usq_done, NCH * n + k - 1)
                    if k == 0:
                        wait(act, gnred_ready, 2 * n)
                    nc.scalar.activation(junk[:, k % 2, :], chunk(us[nxt], k), ACT.Square,
                                         accum_out=gsq[:, k:k + 1]).then_inc(usq_done, 1)

                for s in range(STEPS):
                    def squares(at, late):
                        ks = C_AT.get(at, S_AT.get(at, ())) if p1 else ()
                        for k in ks[len(ks) // 2:] if late else ks[:len(ks) // 2]:
                            (square_xc if at in C_AT else square_u)(k)

                    if p2 and s + 1 < NCH:
                        relu(b, par, s + 1)
                    if p1 and s == NCH:
                        relu(n, nxt, 0)
                    squares(s - 1, True)
                    if p2 and s >= 1:
                        act.wait_ge(e_done, NCH * b + s)
                        j = chunk_of(s - 1)
                        nc.scalar.activation(lg[par][:, SUB * j:SUB * (j + 1)], lgp, ACT.Copy).then_inc(lcopy_done, 1)
                        act.wait_ge(t_done, NCH * b + s)
                        wait(act, stored[(s - 1) % 2], 16 * (8 * b + (s - 1) // 2))
                        nc.scalar.activation(tok[(s - 1) % 2][:].rearrange("p h t c -> p t h c"),
                                             pt[:].rearrange("p (t h c) -> p t h c", t=4, h=2), ACT.Copy).then_inc(tok_done, 1)
                    squares(s, False)
                    if tl and s == 0:
                        act.wait_ge(grp_done, NG * (t + 1))
                        nc.scalar.activation(ta[:], st2[:, 0:SUB], ACT.Square).then_inc(msq_done, 1)
                        act.wait_ge(var2_ready, t + 1)
                        rsqrt_start(v2[:], ta[:], y2[:], 0.0, ln2_done, y2_ready, t + 1)
                    if p1 and s == RSTD_AT:
                        act.wait_ge(sumsq_done, NG * (n + 1))
                        act.wait_ge(const_v, CONST_V)
                        nc.scalar.activation(lnv[:], st1[:, SUB:2 * SUB], ACT.Ln, bias=gt[:, 10:11]).then_inc(lnv_done, 1)
                        act.wait_ge(lnv_done, n + 1)
                        nc.scalar.activation(y0[:], lnv[:], ACT.Exp, scale=-0.5).then_inc(y0_ready, 1)
                    if tl and s in EXP_AT:
                        i = EXP_AT[s]
                        act.wait_ge(top_ready, PIECES * t + i + 1)
                        nc.scalar.activation(piece(lg[nxt], i), piece(lg[nxt], i), ACT.Exp, bias=nmax[:, i:i + 1],
                                             accum_out=cnd[:, 2 * CAND + i:2 * CAND + i + 1]).then_inc(expl_done, 1)
                    if tl and not p2 and s == MERGE_AT:
                        token_rsqrt(0, 0, NB - 1)
                    if tl and s == MERGE_AT + 3:
                        act.wait_ge(bias_ready, t + 1)
                        nc.scalar.activation(tval[:], fval[:], ACT.Exp, bias=gbm[:, 1:2]).then_inc(tval_done, 1)
                        nc.scalar.activation(dexp[:], cval[:, 0:4 * CAND:K], ACT.Exp, bias=gbm[:, 1:2]).then_inc(tval_done, 1)
                    if p1 and s == GN_AT + 1:
                        act.wait_ge(gnv_ready, n + 1)
                        rsqrt_start(gt[:, 3:4], gt[:, 8:9], gt[:, 4:5], 0.0, gnln_done, gny_ready, n + 1)

            nc.scalar.preload_act_table_set("natural_log_exp_and_others")
            iteration(-1, 1, True, False, False)
            iteration(0, 0, True, True, False)
            with act.Fori(0, 3) as i:
                iteration(2 * i + 1, 1, True, True, True)
                iteration(2 * i + 2, 0, True, True, True)
            iteration(7, 1, False, True, True)
            iteration(8, 0, False, False, True)

            token_rsqrt(1, NB - 1, NB)
            act.wait_ge(l1_done, 1)
            nc.scalar.activation(hid[0][:], pc[:], ACT.Gelu).then_inc(gelu_done, 1)

        @block.vector
        def _(dve):
            def iteration(it, par, p1, p2, tl):
                b, n, t = it, it + 1, it - 1
                nxt = 1 - par
                tail = Steps(dve, tail_steps, TAIL_STEPS * t if tl else 0)

                def pix(i):
                    return cnd[:, CAND + K * i:CAND + K * (i + 1)]

                def use_spread(job, i):
                    kind, k = job
                    dve.wait_ge(bc_filled, spread_base(it) + i + 1)
                    stat = bc[i % 2][:]
                    if kind == "L":
                        if k == 0:
                            dve.wait_ge(lcopy_done, NCH * (t + 1))
                        lt = lg[nxt][:, CH * k:CH * (k + 1)]
                        ins = nc.vector.tensor_tensor(lt, lt, stat, ALU.mult)
                    elif kind == "C":
                        ins = nc.vector.tensor_tensor(chunk(us[nxt], k), chunk(xs[nxt], k), stat, ALU.subtract)
                    else:
                        ins = nc.vector.tensor_tensor_reduce(chunk(us[nxt], k), chunk(us[nxt], k), stat, 1.0, 0.0,
                                                             ALU.mult, ALU.add, gsum[:, k:k + 1])
                    ins.then_inc(bc_used, 1)

                for s in range(STEPS):
                    jobs, before = spreads(s, p1, tl)
                    jobs = [(job, before + i) for i, job in enumerate(jobs)]
                    for job in jobs[:len(jobs) // 2]:
                        use_spread(*job)
                    if p2 and s < NCH:
                        dve.wait_ge(d_done, NCH * b + s + 1)
                        dve.wait_ge(s_done, NCH * b + s + 1)
                        xc = chunk(xs[par], s)
                        nc.vector.scalar_tensor_tensor(out=xc, in0=pd[:], scalar=vecs[:, 3:4], in1=xc,
                                                       op0=ALU.add, op1=ALU.add).then_inc(x1_done, 1)
                    for job in jobs[len(jobs) // 2:]:
                        use_spread(*job)
                    if tl and s == 0:
                        dve.wait_ge(msq_done, t + 1)
                        tail(nc.vector.scalar_tensor_tensor(out=v2[:], in0=st2[:, SUB:2 * SUB], scalar=EPS, in1=ta[:],
                                                            op0=ALU.add, op1=ALU.subtract))
                        nc.vector.tensor_scalar(v2[:], v2[:], EPS, None, ALU.max).then_inc(var2_ready, 1)
                        dve.wait_ge(y2_ready, t + 1)
                        newton(tail, v2[:], y2[:], tb[:], 0.0)
                        tail(nc.vector.scalar_tensor_tensor(out=tb[:], in0=tb[:], scalar=1.5, in1=y2[:], op0=ALU.add, op1=ALU.mult))
                        tail(nc.vector.tensor_copy(hi[:], tb[:]))
                        nc.vector.scalar_tensor_tensor(out=rstd2_s[:], in0=hi[:].bitcast(F32), scalar=second[:], in1=tb[:],
                                                       op0=ALU.mult, op1=ALU.add).then_inc(rstd2_ready, 1)
                    if tl and s in MAX_AT:
                        i = MAX_AT[s]
                        dve.wait_ge(bc_used, spread_end(it, "L", 2 * i + 1, p1, tl))
                        hold(dve, spare[:, 0:1])
                        tail(nc.vector.max(cnd[:, K * i:K * i + K], piece(lg[nxt], i)))
                    if tl and s in FIND_AT:
                        i = FIND_AT[s]
                        hold(dve, spare[:, 0:1])
                        tail(nc.vector.max_index(top_i[:], cnd[:, K * i:K * i + K], piece(lg[nxt], i)))
                        tail(nc.vector.tensor_scalar(nmax[:, i:i + 1], cnd[:, K * i:K * i + 1], -1.0, None, ALU.mult))
                        tail(nc.vector.tensor_scalar(top_hi[:], top_i[:], 0xFFFFFF00, None, ALU.bitwise_and))
                        tail(nc.vector.scalar_tensor_tensor(out=pix(i), in0=top_i[:], scalar=rowoff[:], in1=top_hi[:],
                                                            op0=ALU.add, op1=ALU.add))
                        nc.vector.tensor_scalar(pix(i), pix(i), float(2 * PIECE * i), None, ALU.add).then_inc(top_ready, 1)
                    if tl and not p2 and s == MERGE_AT:
                        token_norm(0, 0, NB - 1)
                    if tl and s == MERGE_AT + 2:
                        dve.wait_ge(mrg_done, t + 1)
                        m4 = mrg_p.rearrange("e (r k) -> e r k", r=4)
                        tail(nc.vector.tensor_copy(cpix[:].rearrange("e (r k) -> e r k", r=4), m4[:, :, CAND:2 * CAND]))
                        tail(nc.vector.tensor_copy(csum[:].rearrange("e (r k) -> e r k", r=4), m4[:, :, 2 * CAND:]))
                        tail(nc.vector.tensor_copy(cval[:].rearrange("e (r k) -> e r k", r=4), m4[:, :, 0:CAND]))
                        hold(dve, spare[:, 0:1])
                        tail(nc.vector.max(fval[:], cval[:]))
                        hold(dve, spare[:, 0:1])
                        tail(nc.vector.max_index(fpos[:], fval[:], cval[:]))
                        tail(nc.vector.tensor_tensor(gbm[:, 0:1], fval[:, 0:1], gate_bias[:], ALU.add))
                        nc.vector.tensor_tensor(gbm[:, 1:2], gate_bias[:], gbm[:, 0:1], ALU.subtract).then_inc(bias_ready, 1)
                        tail(nc.vector.tensor_copy(fposf[:], fpos[:]))

                    def pixels(half):
                        ks = slice(K // 2 * half, K // 2 * (half + 1))
                        shape = [NE, K // 2, 4 * CAND]
                        tail(nc.vector.tensor_tensor(onehot, iota[:].unsqueeze(1).broadcast_to(shape),
                                                     fposf[:, ks].unsqueeze(2).broadcast_to(shape), ALU.is_equal))
                        tail(nc.vector.tensor_tensor(onehot, onehot, cpix[:].unsqueeze(1).broadcast_to(shape), ALU.mult))
                        tail(nc.vector.tensor_reduce(pv[:, ks], onehot, AX.X, ALU.add))

                    if p1 and s == GN_AT:
                        dve.wait_ge(bc_used, spread_end(it, "S", NCH - 1, p1, tl))
                        nc.vector.tensor_reduce(gs[:, 0:1], gsum[:], AX.X, ALU.add).then_inc(gnred_ready, 1)
                    if p1 and s == GN_AT + 1:
                        link = Steps(dve, gn_steps, GN_STEPS * n)
                        dve.wait_ge(usq_done, NCH * (n + 1))
                        nc.vector.tensor_reduce(gs[:, 1:2], gsq[:], AX.X, ALU.add).then_inc(gnred_ready, 1)
                        dve.wait_ge(gnps_done, 2 * n + 1)
                        link(nc.vector.tensor_copy(gt[:, 0:2], gn_p))
                        link(nc.vector.scalar_tensor_tensor(out=gt[:, 2:3], in0=gt[:, 0:1], scalar=gt[:, 0:1], in1=gt[:, 1:2],
                                                            op0=ALU.mult, op1=ALU.subtract))
                        link(nc.vector.tensor_scalar(gt[:, 2:3], gt[:, 2:3], -1.0, EPS, ALU.mult, ALU.add))
                        nc.vector.tensor_scalar(gt[:, 3:4], gt[:, 2:3], EPS, None, ALU.max).then_inc(gnv_ready, 1)
                    if tl and s == GN_AT + 1:
                        if not isinstance(it, int) or p1:
                            dve.wait_ge(usq_done, NCH * (n + 1))
                        pixels(0)
                    if p1 and s == GN_AT + 1:
                        dve.wait_ge(gny_ready, n + 1)
                        newton(link, gt[:, 3:4], gt[:, 4:5], gt[:, 5:6], 0.0)
                        link(nc.vector.scalar_tensor_tensor(out=gt[:, 5:6], in0=gt[:, 5:6], scalar=1.5, in1=gt[:, 4:5],
                                                            op0=ALU.add, op1=ALU.mult))
                        link(nc.vector.tensor_tensor(gt[:, 6:7], vecs[:, 0:1], gt[:, 5:6], ALU.mult))
                        nc.vector.scalar_tensor_tensor(out=gt[:, 7:8], in0=gt[:, 0:1], scalar=gt[:, 6:7], in1=vecs[:, 1:2],
                                                       op0=ALU.mult, op1=ALU.subtract).then_inc(gnbias_ready, 1)
                        nc.vector.tensor_scalar(w1n[nxt][:], w1bd[:], gt[:, 6:7], None, ALU.mult).then_inc(w1n_ready, 1)
                        assert link.n == GN_STEPS, link.n
                    if tl and s == GN_AT + 2:
                        pixels(1)
                        dve.wait_ge(tval_done, 2 * (t + 1))
                        tail(nc.vector.tensor_tensor_reduce(djunk[:], dexp[:], csum[:], 1.0, 0.0, ALU.mult, ALU.add, gbm[:, 2:3]))
                        tail(nc.vector.reciprocal(gbm[:, 3:4], gbm[:, 2:3]))
                    if p1 and s == GN_AT + 2:
                        dve.wait_ge(gnps_done, 2 * n + 2)
                        nc.vector.tensor_tensor(b1n[:, nxt:nxt + 1], vecs[:, 2:3], gnb_p, ALU.subtract).then_inc(w1n_ready, 1)
                    if tl and s == GN_AT + 2:
                        nc.vector.tensor_scalar(pv[:, K:2 * K], tval[:], gbm[:, 3:4], None, ALU.mult).then_inc(pv_ready, 1)
                    if tl and s == STEPS - 1:
                        dve.wait_ge(rep_done, t + 1)
                        tail(nc.vector.tensor_tensor(pvm[:], kmask[:].unsqueeze(1).broadcast_to([P, 2 * GATHERS, 4]),
                                                     rep_p.rearrange("p (a k) -> p a k", k=4), ALU.mult))
                        tail(nc.vector.tensor_reduce(pvt[:], pvm[:], AX.X, ALU.add))
                        tail(nc.vector.tensor_scalar(idxf[:], pvt[:, 0:GATHERS], offs[:], None, ALU.add))
                        at = slice(t, t + 1) if isinstance(t, int) else bass.ds(t, 1)
                        tail(nc.vector.tensor_copy(idx_all[:, at, :], idxf[:].unsqueeze(1)))
                        tail(nc.vector.tensor_copy(px_all[:, at, :], pvt[:, 0:GATHERS].unsqueeze(1)))
                        tail(nc.vector.tensor_copy(tv_all[:, at, :], pvt[:, GATHERS:].unsqueeze(1)))
                        nc.vector.tensor_scalar(offs[:], offs[:], float(PIX), None, ALU.add).then_inc(idx_ready, 1)
                        assert tail.n == TAIL_STEPS, tail.n
                    if p1 and s == MEAN_AT:
                        link = Steps(dve, mean_steps, MEAN_STEPS * n)
                        dve.wait_ge(sumx_done, n + 1)
                        link(nc.vector.tensor_copy(hi[:], st1[:, 0:SUB]))
                        nc.vector.scalar_tensor_tensor(out=mean_s[:], in0=hi[:].bitcast(F32), scalar=second[:], in1=st1[:, 0:SUB],
                                                       op0=ALU.mult, op1=ALU.add).then_inc(mean_ready, 1)
                    if p1 and s == RSTD_AT:
                        link = Steps(dve, rstd_steps, RSTD_STEPS * n)
                        dve.wait_ge(y0_ready, n + 1)
                        newton(link, st1[:, SUB:2 * SUB], y0[:], tb[:], EPS_C)
                        link(nc.vector.scalar_tensor_tensor(out=tb[:], in0=tb[:], scalar=1.5, in1=y0[:], op0=ALU.add, op1=ALU.mult))
                        link(nc.vector.tensor_copy(hi[:], tb[:]))
                        nc.vector.scalar_tensor_tensor(out=rstd_s[:], in0=hi[:].bitcast(F32), scalar=second[:], in1=tb[:],
                                                       op0=ALU.mult, op1=ALU.add).then_inc(rstd_ready, 1)

            lns = Steps(dve, ln_steps, 0)

            def token_norm(part, b0, b1):
                dve.wait_ge(rows_in[part], 16 * GATHERS * (b1 - b0))
                n0, n1 = GATHERS * b0, GATHERS * b1
                shape = [P, n1 - n0, C]
                r = rows_all.rearrange("p b g c -> p (b g) c")[:, n0:n1]
                zz = zs.rearrange("p b g c -> p (b g) c")[:, n0:n1]
                q = us[1][:, n0 * C:n1 * C].rearrange("p (n c) -> p n c", c=C)
                mean, var, y, a, rs, ws = (tr[:, i, n0:n1] for i in range(6))
                lns(nc.vector.tensor_reduce(mean, r, AX.X, ALU.add))
                lns(nc.vector.tensor_scalar(mean, mean, 1.0 / C, None, ALU.mult))
                lns(nc.vector.tensor_tensor(zz, r, mean.unsqueeze(2).broadcast_to(shape), ALU.subtract))
                lns(nc.vector.tensor_tensor(q, zz, zz, ALU.mult))
                lns(nc.vector.tensor_reduce(var, q, AX.X, ALU.add))
                nc.vector.tensor_scalar(var, var, 1.0 / C, EPS, ALU.mult, ALU.add).then_inc(rvar_ready, 1)
                dve.wait_ge(ry_ready, part + 1)
                newton(lns, var, y, a, 0.0)
                lns(nc.vector.scalar_tensor_tensor(out=rs, in0=a, scalar=1.5, in1=y, op0=ALU.add, op1=ALU.mult))
                lns(nc.vector.tensor_tensor(ws, rs, tv_all[:, b0:b1].rearrange("p b g -> p (b g)"), ALU.mult))
                nc.vector.tensor_tensor(zz, zz, ws.unsqueeze(2).broadcast_to(shape), ALU.mult).then_inc(z_ready, 1)

            cv = Steps(dve, const_steps, 0)
            nc.vector.memset(w1bd[:], 0.0)
            nc.vector.memset(w2bd[:], 0.0)
            cv(nc.vector.memset(gbd[:], 0.0))
            nc.vector.memset(gt[:, 0:10], 0.0).then_inc(const_d, 1)
            for r in range(4):
                nc.vector.memset(rowoff[32 * r:32 * r + 32, :], float(SUB * (r // 2) + HW * (r % 2)))
            nc.vector.memset(offs[:], 0.0)
            nc.vector.memset(gt[:, 10:11], EPS_C)
            cv(nc.vector.memset(stat_w[:], 0.0))
            sw = stat_w[:].rearrange("p q m -> p (q m)")
            for h in range(HALVES):
                for d in range(2):
                    ins = nc.vector.memset(sw[C * h:C * h + C, h + 16 * d:h + 16 * d + 34 * 7 + 1:34], 1.0 / C)
            cv(ins)
            dve.wait_ge(const_p, CONST_P)
            nc.vector.tensor_copy(spread[:], lg[0][:, 0:1024])
            nc.vector.tensor_copy(rep[:].rearrange("e (k f) -> e k f", k=4),
                                  ident[0:NE, 0:NE].unsqueeze(1).broadcast_to([NE, 4, NE]))
            nc.vector.tensor_reduce(kmask[:], ident[:].rearrange("p (k e) -> p k e", k=4), AX.X, ALU.add)
            cv(nc.vector.tensor_reduce(esel[:], ident[:].rearrange("p (k e) -> p e k", k=4), AX.X, ALU.add))
            cv(nc.vector.memset(cen[:], 0.0))
            for h in range(HALVES):
                ins = nc.vector.memset(cen[C * h:C * h + C, C * h:C * h + C], 1.0 / C)
            cv(ins)
            nc.vector.tensor_tensor(cen[:], ident[:], cen[:], ALU.subtract).then_inc(const_v, 1)
            dve.wait_ge(w_in, 16 * 15)
            dve.wait_ge(const_t, 1)
            nc.vector.tensor_copy(gcen[:], pe_b[:, 0:C]).then_inc(const_v, 1)
            dve.wait_ge(const_v, CONST_V + 1)

            iteration(-1, 1, True, False, False)
            iteration(0, 0, True, True, False)
            with dve.Fori(0, 3) as i:
                iteration(2 * i + 1, 1, True, True, True)
                iteration(2 * i + 2, 0, True, True, True)
            iteration(7, 1, False, True, True)
            iteration(8, 0, False, False, True)

            token_norm(1, NB - 1, NB)
            lns(nc.vector.memset(pooled, 1.0))
            dve.wait_ge(pool_done, 1)
            nc.vector.tensor_copy(pooled[0:C, :, :].rearrange("c e b -> c b e"),
                                  bc[0][0:C, 0:NE * NB].rearrange("c (b e) -> c b e", b=NB)).then_inc(pooled_ready, 1)

            dve.wait_ge(pex_done, 1)
            nc.vector.tensor_copy(tb[0:C, 0:NE], pt[0:C, 0:NE]).then_inc(ebias_ready, 1)
            dve.wait_ge(ebias_ready, 1)
            dve.wait_ge(l2_done, 1)
            for kk in range(4):
                ins = nc.vector.tensor_tensor(
                    us[1][0:C, 0:NB * P].rearrange("o (b k e) -> o k e b", b=NB, k=4)[:, kk],
                    tb[0:C, 0:NE].unsqueeze(2).broadcast_to([C, NE, NB]),
                    pd[0:C, 0:NE * NB].rearrange("o (e b) -> o e b", b=NB), ALU.add)
            ins.then_inc(eo_ready, 1)
            dve.wait_ge(eo_ready, 1)
            dve.wait_ge(usq_done, NCH * NB)
            ins = nc.vector.memset(ones, 1.0)
            for b in range(NB):
                dve.wait_ge(ob_done, b + 1)
                if b >= 1:
                    dve.wait_ge(add_done, b)
                for g in range(GATHERS):
                    nc.vector.tensor_scalar(hid[0][:, P * g:P * g + P], ident[:], px_all[:, b, g:g + 1], None, ALU.mult)
                    ins = nc.vector.tensor_scalar(z[:, g, :], pt[:, 0:C], tv_all[:, b, g:g + 1], None, ALU.mult)
                ins.then_inc(diag_ready, 1)
                dve.wait_ge(pxr_done, b + 1)
                for g in range(GATHERS):
                    ins = nc.vector.tensor_scalar(sqc[:, g, 0:GATHERS * P], bc[0][:, 0:GATHERS * P], px_all[:, b, g:g + 1],
                                                  None, ALU.is_equal)
                ins.then_inc(eq_ready, 1)
                dve.wait_ge(add_done, b + 1)
                rv = rows_all[:, b].rearrange("p g c -> p (g c)")
                nc.vector.tensor_tensor(rv, rv, bc[1][:, 0:GATHERS * C], ALU.add).then_inc(row_ready, 1)

        @block.gpsimd
        def _(pool):
            cp = Steps(pool, pool_steps, 0)
            nc.gpsimd.memset(ident[:], 0.0)
            nc.gpsimd.memset(gsel[:], 1.0 / (GN_GROUP * PIX))
            nc.gpsimd.memset(lg[0][:, 0:1024], 0.0)
            nc.gpsimd.memset(second[:], -1.0)
            nc.gpsimd.iota(iota[:], pattern=[[1, 4 * CAND]], base=0, channel_multiplier=0, allow_small_or_imprecise_dtypes=True)
            cp(nc.gpsimd.memset(lg[1][:, 0:1], 0.0))
            cp(nc.gpsimd.affine_select(out=ident[:], in_=ident[:], compare_op=ALU.not_equal, fill=1.0, base=0,
                                       pattern=[[-1, P]], channel_multiplier=1))
            for q in range(4):
                for copy in range(2):
                    v = lg[0][32 * q:32 * q + 32, 0:1024].rearrange("p (r y) -> p r y", r=16)
                    cp(nc.gpsimd.affine_select(out=v, in_=v, compare_op=ALU.not_equal, fill=1.0, base=-16 * copy,
                                               pattern=[[-1, 16], [0, C]], channel_multiplier=1))
                v = second[32 * q:32 * q + 32, :]
                cp(nc.gpsimd.affine_select(out=v, in_=v, compare_op=ALU.is_ge, fill=0.0, base=-16,
                                           pattern=[[0, 1]], channel_multiplier=1))
            for h in range(HALVES):
                v = gsel[C * h:C * h + C, :].rearrange("p (a g i) -> p a g i", a=2, g=C // GN_GROUP)
                pat = [[0, 2], [-GN_GROUP, C // GN_GROUP], [0, GN_GROUP]]
                cp(nc.gpsimd.affine_select(out=v, in_=v, compare_op=ALU.is_ge, fill=0.0, base=0, pattern=pat,
                                           channel_multiplier=1))
                pat = [[0, 2], [GN_GROUP, C // GN_GROUP], [0, GN_GROUP]]
                cp(nc.gpsimd.affine_select(out=v, in_=v, compare_op=ALU.is_ge, fill=0.0, base=GN_GROUP - 1, pattern=pat,
                                           channel_multiplier=-1))
            nc.gpsimd.memset(lg[1][:, 0:1], 0.0).then_inc(const_p, 1)

            def iteration(it, par, p1, p2, tl):
                b, n, t = it, it + 1, it - 1
                nxt = 1 - par
                for s in range(STEPS):
                    if p2 and s < NCH:
                        pool.wait_ge(x1_done, NCH * b + s + 1)
                        wait(pool, grp_done, NG * b + s // GRP)
                        xc = chunk(xs[par], s)
                        nc.gpsimd.tensor_tensor(sqx[:, s % GRP, :], xc, xc, ALU.mult).then_inc(sqx_done, 1)
                    if p1:
                        for k in ADD_AT.get(s, ()):
                            pool.wait_ge(bc_used, spread_end(it, "S", k, p1, tl))
                            nc.gpsimd.tensor_tensor(chunk(xs[nxt], k), chunk(xs[nxt], k), chunk(us[nxt], k),
                                                    ALU.add).then_inc(s_done, 1)
            iteration(-1, 1, True, False, False)
            iteration(0, 0, True, True, False)
            with pool.Fori(0, 3) as i:
                iteration(2 * i + 1, 1, True, True, True)
                iteration(2 * i + 2, 0, True, True, True)
            iteration(7, 1, False, True, True)
            iteration(8, 0, False, False, True)
            for q in range(2):
                pool.wait_ge(stored[q], 16 * (NCH // 2) * NB)
            pool.wait_ge(grp_done, NG * NB)
            for b in range(NB):
                if b in (0, NB - 1):
                    pool.wait_ge(idx_ready, NB - 1 if b == 0 else NB)
                for g in range(GATHERS):
                    nc.gpsimd.indirect_dma_start(
                        rows_all[:, b, g, :], None, out_rows,
                        bass.IndirectOffsetOnAxis(ap=idx_all[:, b, g:g + 1], axis=0)).then_inc(rows_in[b == NB - 1], 16)
            for b in range(NB):
                pool.wait_ge(row_ready, b + 1)
                for g in range(GATHERS):
                    wait(pool, scattered, 16 * (GATHERS * b + g))
                    nc.gpsimd.indirect_dma_start(
                        out_rows, bass.IndirectOffsetOnAxis(ap=idx_all[:, b, g:g + 1], axis=0),
                        rows_all[:, b, g, :], None).then_inc(scattered, 16)
            pool.wait_ge(scattered, 16 * GATHERS * NB)


def kernel(x, L0_conv_gn_w, L0_conv_gn_b, L0_conv_w1, L0_conv_b1, L0_conv_w2, L0_conv_b2,
           L0_ffn_gate_w, L0_ffn_gate_b, L0_ffn_weight1, L0_ffn_weight2):
    import numpy as np
    import concourse.bacc as bacc
    from concourse.bass_utils import run_bass_kernel_spmd

    ins = {
        "x": np.ascontiguousarray(x).reshape(NB, C, PIX),
        "gn_w": L0_conv_gn_w, "gn_b": L0_conv_gn_b,
        "w1T": np.asarray(L0_conv_w1).T, "b1": L0_conv_b1,
        "w2T": np.asarray(L0_conv_w2).T, "b2": L0_conv_b2,
        "gateT": np.asarray(L0_ffn_gate_w).T, "gate_b": L0_ffn_gate_b,
        "e_w1": L0_ffn_weight1, "e_w2": L0_ffn_weight2,
    }
    nc = bacc.Bacc("TRN2", target_bir_lowering=False, num_devices=1)
    arrays, args = {}, []
    for name, a in ins.items():
        a = np.ascontiguousarray(a)
        arrays[f"in_{name}"] = a
        args.append(nc.dram_tensor(f"in_{name}", a.shape, mybir.dt.from_np(a.dtype), kind="ExternalInput").ap())
    args.append(nc.dram_tensor("out_rows", (NB, PIX, C), F32, kind="ExternalOutput").ap())
    mk_metaformer_kernel(nc, *args)
    r = run_bass_kernel_spmd(nc, [arrays], core_ids=[0])
    got = r.results[0]["out_rows"]
    return np.ascontiguousarray(got.transpose(0, 2, 1)).reshape(NB, C, 128, 128)
```

```python
from contextlib import ExitStack

import concourse.bass as bass
from concourse import mybir

F32 = mybir.dt.float32
F32R = mybir.dt.float32r
U32 = mybir.dt.uint32
ALU = mybir.AluOpType
ACT = mybir.ActivationFunctionType
AX = mybir.AxisListType

P = 128
C = 64
HALVES = 2
NB = 8
PIX = 128 * 128
HW = PIX // HALVES
CH = 512
SUB = 256
NCH = HW // CH
GRP = 4
NG = NCH // GRP
NE = 32
K = 8
HID = 256
EPS_C = 1e-6
EPS = 1e-5
GN_GROUP = 8
GATHERS = K * NE // P
ORDER = (0, 1, 5, 2, 3, 6, 4, 7)
SCATTERS = ((0, 0), (1, 0), (0, 1), (1, 1), (5, 0), (2, 0), (5, 1), (2, 1),
            (3, 0), (6, 0), (3, 1), (6, 1), (4, 0), (7, 0), (4, 1), (7, 1))
LOOPED = 5
PIECES = 4
PIECE = HW // 2 // PIECES
CAND = PIECES * K
MRG = 2 * CAND + PIECES

STEPS = NCH + 1
L_AT = {1: (0, 1), 2: (2, 3), 3: (4, 5), 8: (6, 7)}
C_AT = {s: tuple(range(GRP * (s - 4), GRP * (s - 3))) for s in range(4, 8)}
S_AT = {9: (0, 1), 10: (2, 3, 4, 5), 11: (6, 7, 8, 9), 12: (10, 11, 12, 13), 13: (14, 15)}
ADD_AT = {10: (0, 1), 11: (2, 3), 12: (4, 5), 13: (6, 7), 14: (8,), 15: (9,), 16: (10, 11)}
LATE_ADD_AT = {0: 12, 1: 13, 2: 14, 3: 15}
MAX_AT, FIND_AT, EXP_AT = {1: 0, 4: 1, 6: 2, 8: 3}, {1: 0, 5: 1, 7: 2, 9: 3}, {2: 0, 6: 1, 8: 2, 10: 3}
SUMX_AT = {0: (0, 1), 1: (2,), 2: (3,)}
PAIR_AT, NORM_AT = (10, 12, 14), (8, 9, 10)
MEAN_AT, RSTD_AT, GN_AT, MERGE_AT = 3, 8, 13, 11
NL, NSPREAD = 2 * PIECES, 2 * NCH


def place(b):
    return (b % 2, b // 2) if b < LOOPED else (b - LOOPED + 2, 0)


def spreads(s, p1, tl):
    def of(t):
        return ([("L", k) for k in L_AT.get(t, ())] if tl else []) + \
               ([("C", k) for k in C_AT.get(t, ())] + [("S", k) for k in S_AT.get(t, ())] if p1 else [])
    return of(s), sum(len(of(t)) for t in range(s))


def spread_pairs(it):
    if isinstance(it, int):
        return ((it + 1) * NSPREAD if it < 1 else
                2 * NSPREAD + (NL + NSPREAD) * min(it - 1, 6) + NL * max(it - 7, 0)) // 2
    return NSPREAD + (NL + NSPREAD) // 2 * (it - 1)


def chunk_of(s):
    return GRP * (s % GRP) + s // GRP


def spread_at(it, kind, k, p1, tl):
    every = [job for s in range(STEPS) for job in spreads(s, p1, tl)[0]]
    i = every.index((kind, k))
    return i % 2, spread_pairs(it) + i // 2 + 1


def mk_metaformer_kernel(nc, x, gn_w, gn_b, w1T, b1, w2T, b2, gateT, gate_b, e_w1, e_w2, *outs):
    ctx = ExitStack()
    with ctx:
        def sb(name, shape, dt=F32):
            return ctx.enter_context(nc.sbuf_tensor(name, shape, dt))

        def bank(name):
            return ctx.enter_context(nc.psum_tensor(name, [P, CH], F32))

        def sem(name):
            return ctx.enter_context(nc.semaphore(name))

        xs = [sb(f"xs{i}", [P, HW]) for i in range(2)]
        us = [sb(f"us{i}", [P, HW]) for i in range(2)]
        lg = [sb(f"lg{i}", [P, HW // 2]) for i in range(2)]
        hid = [sb(f"hid{i}", [P, CH]) for i in range(2)]
        tok = [sb(f"tok{i}", [P, HALVES, GRP, C]) for i in range(2)]
        sqc = sb("sqc", [P, GRP, CH])
        sqx = sb("sqx", [P, GRP, CH])
        junk = sb("junk", [P, 2, CH], mybir.dt.bfloat16)

        ident = sb("ident", [P, P])
        stat_w = sb("stat_w", [P, 8, 32])
        spread = sb("spread", [P, 16 * 64], F32R)
        second = sb("second", [P, 1])
        gsel = sb("gsel", [P, P])
        w1bd = sb("w1bd", [P, P])
        w1n = [sb(f"w1n{i}", [P, P]) for i in range(2)]
        cen = w1n[1]
        w2bd = sb("w2bd", [P, P])
        gbd = sb("gbd", [P, C])
        gcen = sb("gcen", [P, C])
        vecs = sb("vecs", [P, 4])
        gate_bias = sb("gate_bias", [NE, 1])
        kmask = sb("kmask", [P, 4])
        esel = sb("esel", [P, NE])
        rep = sb("rep", [NE, P])
        iota = sb("iota", [NE, 4 * CAND])
        rowoff = sb("rowoff", [P, 1])

        hi = sb("hi", [P, SUB], F32R)
        mean_s = sb("mean_s", [P, SUB], F32R)
        rstd_s = sb("rstd_s", [P, SUB], F32R)
        rstd2_s = sb("rstd2_s", [P, SUB], F32R)
        lnv, y0, ta, tb = (sb(n, [P, SUB]) for n in ("lnv", "y0", "ta", "tb"))
        v2, y2 = lnv, y0
        gsum = sb("gsum", [P, NCH])
        gsq = sb("gsq", [P, NCH])
        gs = sb("gs", [P, 2])
        gt = sb("gt", [P, 12])
        b1n = sb("b1n", [P, 2])
        spare = sb("spare", [P, 1])

        cnd = sb("cnd", [P, MRG])
        top_i = sb("top_i", [P, K], U32)
        top_hi = sb("top_hi", [P, K], U32)
        nmax = sb("nmax", [P, PIECES])
        cval = sb("cval", [NE, 4 * CAND])
        cpix = sb("cpix", [NE, 4 * CAND])
        csum = sb("csum", [NE, 4 * PIECES])
        fval = sb("fval", [NE, K])
        fpos = sb("fpos", [NE, K], U32)
        fposf = sb("fposf", [NE, K])
        onehots = [x.rearrange("p (k n) -> p k n", k=K // 2)
                   for x in (junk[0:NE].rearrange("p a n -> p (a n)").bitcast(F32), sqc[0:NE, 0, :])]
        gbm = sb("gbm", [NE, 4])
        tval = sb("tval", [NE, K])
        dexp = sb("dexp", [NE, 4 * PIECES])
        djunk = sb("djunk", [NE, 4 * PIECES])
        pv = sb("pv", [NE, 2 * K])
        pvm = sb("pvm", [P, 2 * GATHERS, 4])
        pvt = sb("pvt", [P, 2 * GATHERS])
        offs = sb("offs", [P, 1])
        idxf = sb("idxf", [P, GATHERS])
        idx_all = sb("idx_all", [P, NB, GATHERS], U32)
        px_all = sb("px_all", [P, NB, GATHERS])
        tv_all = sb("tv_all", [P, NB, GATHERS])
        tr = sb("tr", [P, 6, NB * GATHERS])

        def batches(ap):
            return ap.rearrange("p (b g c) -> p b g c", b=NB, g=GATHERS)
        sqc_f = sqc[:].rearrange("p g n -> p (g n)")
        rows_all = batches(sqc_f[:, 0:NB * GATHERS * C])
        zs = batches(sqc_f[:, 2 * CH:2 * CH + NB * GATHERS * C])
        ones = gsel
        ew1 = us[0][0:C + 1, :].rearrange("d (e n) -> d e n", e=NE)
        ew2 = xs[0][:, 0:NE * 2 * C].rearrange("p (e k o) -> p e k o", e=NE, k=2)
        eb2 = gbd[0:NE, :]
        eq = xs[0][:, HW // 2:HW].rearrange("p (b f i) -> p b f i", b=NB, f=GATHERS)
        pool_f = lg[0][0:C + 1, 0:NE * NB + 3 * NB]
        zsq = [eq[:, 6:8].rearrange("p b f i -> p (b f i)"), lg[0][:, CH:2 * CH]]
        diags = [eq[:, 7 - p % 2].rearrange("p f i -> p (f i)") for p in range(3)] + [lg[0][:, 2 * CH:3 * CH]]
        hg = us[1][:, 0:4 * CH]
        ht = us[1][:, 4 * CH:5 * CH]
        eot = us[1][:, 5 * CH:7 * CH]
        zc = us[1][:, 7 * CH:9 * CH].rearrange("p (b g c) -> p b g c", b=NB, g=GATHERS)
        id2 = gcen
        eb2t = tb[:, 0:NE]

        bc = [bank(f"bc{i}") for i in range(2)]
        pc, pd, pe_b, pt = bank("pc"), bank("pd"), bank("pe_b"), bank("pt")
        st1, st2 = bank("st1"), bank("st2")
        lgp = pe_b[:, 0:SUB]
        mrg_p = st1[0:NE, 0:4 * MRG]
        rep_p = st1[:, 300:300 + 2 * K]
        gn_p = st1[:, 340:342]
        gnb_p = st1[:, 344:345]
        h_banks, t_banks, add_banks = (pd, pe_b, pt, st2), (bc[0], pc, st1, bc[1]), (pt, st2)

        w_in, x_in = sem("w_in"), [sem(f"x_in{m}") for m in range(NG)]
        const_p, const_v, const_d, const_t = sem("const_p"), sem("const_v"), sem("const_d"), sem("const_t")
        sumx_done, mean_ready, mean_steps = sem("sumx_done"), sem("mean_ready"), sem("mean_steps")
        bc_filled, bc_used = ([sem(f"bc_{what}{i}") for i in range(2)] for what in ("filled", "used"))
        sqc_done, sumsq_done = sem("sqc_done"), sem("sumsq_done")
        lnv_done, y0_ready, rstd_steps, rstd_ready = (sem(n) for n in ("lnv_done", "y0_ready", "rstd_steps", "rstd_ready"))
        usq_done, s_done = sem("usq_done"), sem("s_done")
        gn_steps, gnred_ready, gnps_done, gnv_ready = (sem(n) for n in ("gn_steps", "gnred_ready", "gnps_done", "gnv_ready"))
        gnln_done, gny_ready, gnbias_ready, w1n_ready = (sem(n) for n in ("gnln_done", "gny_ready", "gnbias_ready", "w1n_ready"))
        c_done, h_done, d_done, x1_done = (sem(n) for n in ("c_done", "h_done", "d_done", "x1_done"))
        e_done, lcopy_done, t_done, tok_done = (sem(n) for n in ("e_done", "lcopy_done", "t_done", "tok_done"))
        sqx_done, grp_done = sem("sqx_done"), sem("grp_done")
        stored = [sem(f"stored{i}") for i in range(2)]
        msq_done, var2_ready, ln2_done, y2_ready = (sem(n) for n in ("msq_done", "var2_ready", "ln2_done", "y2_ready"))
        tail_steps, rstd2_ready = sem("tail_steps"), sem("rstd2_ready")
        top_ready, expl_done, mrg_done, bias_ready = (sem(n) for n in ("top_ready", "expl_done", "mrg_done", "bias_ready"))
        tval_done, pv_ready, rep_done, idx_ready = (sem(n) for n in ("tval_done", "pv_ready", "rep_done", "idx_ready"))
        rows_in = [sem("rows_in0"), sem("rows_in1")]
        scattered = [sem(f"scattered{i}") for i in range(len(outs))]
        late_ready, zero_ready, ht_ready = sem("late_ready"), sem("zero_ready"), sem("ht_ready")
        t2_done = sem("t2_done")
        ln_steps, rvar_ready, rln_done, ry_ready = (sem(n) for n in ("ln_steps", "rvar_ready", "rln_done", "ry_ready"))
        z_ready, pool_done, pooled_ready = (sem(n) for n in ("z_ready", "pool_done", "pooled_ready"))
        ew_in, l1_done, gelu_done, l2_done = (sem(n) for n in ("ew_in", "l1_done", "gelu_done", "l2_done"))
        eo_ready, ob_done, diag_ready = (sem(n) for n in ("eo_ready", "ob_done", "diag_ready"))
        pxr_done, eq_ready, z_done, add_done, row_ready = (
            sem(n) for n in ("pxr_done", "eq_ready", "z_done", "add_done", "row_ready"))
        pex_done, ebias_ready = sem("pex_done"), sem("ebias_ready")
        pool_steps, const_steps = sem("pool_steps"), sem("const_steps")

        x_h = x.rearrange("b c (h k m n) -> b h c k m n", h=HALVES, k=GRP, m=NG)
        out_ts = [o.rearrange("b (h j p t) c -> b j p h (t c)", h=HALVES, j=NCH, p=P) for o in outs]
        out_rows = [o.rearrange("b p c -> (b p) c") for o in outs]

        MEAN_STEPS, RSTD_STEPS, GN_STEPS, TAIL_STEPS = 1, 4, 7, 38

        def chunk(buf, s):
            j = chunk_of(s)
            return buf[:, CH * j:CH * (j + 1)]

        def piece(buf, i):
            return buf[:, PIECE * i:PIECE * (i + 1)]

        def used(eng, it, kind, k, p1, tl):
            bank, count = spread_at(it, kind, k, p1, tl)
            eng.wait_ge(bc_used[bank], count)

        def first(jobs):
            return len(jobs) // 2 if len(jobs) >= 4 else 0

        def wait(eng, s, value):
            if not isinstance(value, int) or value > 0:
                eng.wait_ge(s, value)

        def hold(eng, cell):
            eng.tensor_tensor(cell, second[:, 0:1], second[:, 0:1], ALU.mult)

        class Steps:
            def __init__(self, eng, s, base):
                self.eng, self.sem, self.base, self.n = eng, s, base, 0

            def __call__(self, ins):
                self.n += 1
                ins.then_inc(self.sem, 1)
                self.eng.wait_ge(self.sem, self.base + self.n)

        def newton(link, v, y, a, eps):
            link(nc.vector.scalar_tensor_tensor(out=a, in0=v, scalar=eps, in1=y, op0=ALU.add, op1=ALU.mult))
            link(nc.vector.scalar_tensor_tensor(out=a, in0=a, scalar=-0.5, in1=y, op0=ALU.mult, op1=ALU.mult))

        block = ctx.enter_context(nc.Block())

        @block.sync
        def _(sp):
            def load(b, m, slot):
                for h in range(HALVES):
                    dst = xs[slot][C * h:C * h + C, :].rearrange("c (k m n) -> c k m n", k=GRP, m=NG)[:, :, m, :]
                    src = x_h[b, h, :, :, m, :] if isinstance(b, int) else \
                        x_h[bass.ds(b, 1), h, :, :, m, :].rearrange("a c k n -> (a c) k n")
                    sp.dma_start(dst, src).then_inc(x_in[m], 16)

            for m in range(NG):
                load(0, m, 0)
            for vec, src in enumerate((gn_w, gn_b, b1, b2)):
                for h in range(HALVES):
                    sp.dma_start(vecs[C * h:C * h + C, vec:vec + 1], src.rearrange("(c a) -> c a", a=1)).then_inc(w_in, 16)
            sp.dma_start(gate_bias[:], gate_b.rearrange("(e a) -> e a", a=1)).then_inc(w_in, 16)
            sp.wait_ge(const_d, 1)
            for h in range(HALVES):
                r = slice(C * h, C * h + C)
                sp.dma_start(w1bd[r, r], w1T).then_inc(w_in, 16)
                sp.dma_start(w2bd[r, r], w2T).then_inc(w_in, 16)
                sp.dma_start(gbd[r, NE * h:NE * h + NE], gateT).then_inc(w_in, 16)
            sp.wait_ge(sumx_done, 1)
            for m in range(NG):
                load(1, m, 1)

            def load_weights(part):
                e = slice(NE // 4 * part, NE // 4 * (part + 1))
                if part == 0:
                    sp.wait_ge(grp_done, 7 * NG)
                    sp.dma_start(eb2, e_w2[:, HID, :]).then_inc(ew_in, 16)
                sp.dma_start(ew1[:, e], e_w1[e].rearrange("e d n -> d e n")).then_inc(ew_in, 16)
                for k in range(2):
                    sp.dma_start(ew2[:, e, k, :], e_w2[e, k * P:(k + 1) * P, :].rearrange("e p o -> p e o")).then_inc(ew_in, 16)

            def iteration(it, par, loads, i=None):
                for s in range(NCH + 1):
                    if isinstance(it, int) and it == NB - 1 and s in (2, 5, 8, 11):
                        load_weights((s - 2) // 3)
                    if s < NCH:
                        sp.wait_ge(tok_done, it * NCH + s + 1)
                        if isinstance(it, int):
                            q, at = place(it)
                            dst = out_ts[q][at, chunk_of(s)]
                        else:
                            dst = out_ts[par][bass.ds(i + 1 - par, 1), chunk_of(s)].rearrange("a p h n -> (a p) h n")
                        sp.dma_start(dst, tok[s % 2][:].rearrange("p h t c -> p h (t c)")).then_inc(stored[s % 2], 16)
                    if loads and (s > GRP and s % GRP == 1 or s == NCH):
                        m = NG - 1 if s == NCH else s // GRP - 1
                        sp.wait_ge(grp_done, it * NG + m + 1)
                        load(it + 2, m, par)

            iteration(0, 0, True)
            with sp.Fori(0, 2) as i:
                iteration(2 * i + 1, 1, True, i)
                iteration(2 * i + 2, 0, True, i)
            iteration(5, 1, True)
            iteration(6, 0, False)
            iteration(7, 1, False)

        @block.tensor
        def _(pe):
            def sub_sum(dst, src, s, sub, start):
                c, q = s % GRP, 2 * (s // GRP) + sub
                col = CH * chunk_of(s) if src.shape[-1] == HW else CH * (s % GRP)
                return pe.matmul(dst[32 * c:32 * c + 32], stat_w[:, q, :], src[:, col + SUB * sub:col + SUB * sub + SUB],
                                 start=start, stop=True, skip_group_check=True)

            def sum_group(dst, src, m, first):
                for sub in range(2):
                    for c in range(GRP):
                        mm = sub_sum(dst, src, GRP * m + c, sub, first and m == 0 and sub == 0)
                return mm

            def spread_chunk(dst, stat, j):
                c = j // GRP
                for sub in range(2):
                    w = 2 * C * (2 * (j % GRP) + sub)
                    mm = pe.matmul(dst[:, SUB * sub:SUB * sub + SUB], spread[32 * c:32 * c + 32, w:w + 2 * C],
                                   stat[32 * c:32 * c + 32, :], start=True, stop=True)
                return mm

            def iteration(it, par, p1, p2, tl):
                b, n, t = it, it + 1, it - 1
                nxt = 1 - par

                def spread_stat(job, i, s):
                    kind, k = job
                    if kind == "L" and k == 0:
                        pe.wait_ge(rstd2_ready, t + 1)
                    if kind == "C" and k == 0:
                        pe.wait_ge(mean_ready, n + 1)
                        if not p2:
                            pe.wait_ge(const_v, 2)
                    if kind == "S" and k == 0:
                        pe.wait_ge(rstd_ready, n + 1)
                    wait(pe, bc_used[i % 2], spread_pairs(it) + i // 2)
                    if kind == "L":
                        for h in range(2):
                            j = 2 * k + h
                            c, w = j // GRP, 4 * C * (j % GRP)
                            mm = pe.matmul(bc[i % 2][:, SUB * h:SUB * h + SUB], spread[32 * c:32 * c + 32, w:w + 4 * C:2],
                                           rstd2_s[32 * c:32 * c + 32, :], start=True, stop=True)
                    else:
                        mm = spread_chunk(bc[i % 2], mean_s if kind == "C" else rstd_s, chunk_of(k))
                    mm.then_inc(bc_filled[i % 2], 1)

                def conv1(b, par, s):
                    if s == 0:
                        pe.wait_ge(w1n_ready, 2 * b + 1)
                    wait(pe, h_done, NCH * b + s)
                    pe.matmul(pc[:], w1n[par][:], chunk(us[par], s), start=True, stop=True).then_inc(c_done, 1)

                def conv2(s):
                    pe.wait_ge(h_done, NCH * b + s + 1)
                    wait(pe, x1_done, NCH * b + s)
                    pe.matmul(pd[:], w2bd[:], hid[s % 2][:], start=True, stop=True).then_inc(d_done, 1)

                def logits_and_tokens(s):
                    pe.wait_ge(x1_done, NCH * b + s + 1)
                    wait(pe, lcopy_done, NCH * b + s)
                    col = CH * chunk_of(s)
                    for slot in range(2):
                        mm = pe.matmul(lgp[C * slot:C * slot + C], gcen[:],
                                       xs[par][:, col + SUB * slot:col + SUB * slot + SUB], start=True, stop=True)
                    mm.then_inc(e_done, 1)
                    wait(pe, tok_done, NCH * b + s)
                    for k in range(4):
                        mm = pe.transpose(pt[:, P * k:P * k + P], xs[par][:, col + k:col + CH:4], ident[:])
                    mm.then_inc(t_done, 1)

                for s in range(STEPS):
                    jobs, before = spreads(s, p1, tl)
                    jobs = [(job, before + i, s) for i, job in enumerate(jobs)]
                    if p2 and s + 1 < NCH:
                        conv1(b, par, s + 1)
                    for job in jobs[:first(jobs)]:
                        spread_stat(*job)
                    if p2 and not p1 and s in PAIR_AT:
                        spread_pixels(PAIR_AT.index(s))
                    if not p1 and not p2 and s == 4:
                        pe.wait_ge(ew_in, 16 * 13)
                        pe.wait_ge(tok_done, NCH * NB)
                        for h in range(HALVES):
                            mm = pe.matmul(pt[C * h:C * h + C, 0:NE], eb2, ident[0:NE, 0:NE], start=True, stop=True)
                        mm.then_inc(pex_done, 1)
                        pe.wait_ge(z_ready, 1)
                        pe.wait_ge(h_done, NCH * NB)
                        pool_rows(0, 6)
                    if p2 and s < NCH:
                        conv2(s)
                    if p2 and s >= 1:
                        logits_and_tokens(s - 1)
                    if p1 and s == GN_AT + 1:
                        pe.wait_ge(gnred_ready, 2 * (n + 1))
                        if not p2:
                            pe.wait_ge(const_p, 2)
                            pe.wait_ge(w_in, 16 * 15)
                        pe.matmul(gn_p, gsel[:], gs[:], start=True, stop=True).then_inc(gnps_done, 1)
                    if tl and s == MERGE_AT + 1:
                        pe.wait_ge(top_ready, PIECES * (t + 1))
                        pe.wait_ge(expl_done, PIECES * (t + 1))
                        if p1:
                            pe.wait_ge(rstd_ready, n + 1)
                        for r in range(4):
                            mm = pe.matmul(mrg_p[:, MRG * r:MRG * r + MRG], ident[:, NE * r:NE * r + NE], cnd[:],
                                           start=True, stop=True)
                        mm.then_inc(mrg_done, 1)
                    for job in jobs[first(jobs):]:
                        spread_stat(*job)
                    if p1 and s - 1 in C_AT:
                        m = s - 1 - min(C_AT)
                        pe.wait_ge(sqc_done, NCH * n + GRP * (m + 1))
                        sum_group(st1[:, SUB:2 * SUB], sqc[:].rearrange("p g n -> p (g n)"), m, True).then_inc(sumsq_done, 1)
                    if p2 and s >= GRP and s % GRP == 0:
                        if s == GRP and tl:
                            pe.wait_ge(var2_ready, t + 1)
                        sum_group(st2[:, 0:SUB], xs[par][:], s // GRP - 1, True)
                    if p1 and s == GN_AT + 3:
                        pe.wait_ge(gnbias_ready, n + 1)
                        pe.matmul(gnb_p, w1bd[:], gt[:, 7:8], start=True, stop=True).then_inc(gnps_done, 1)
                    if tl and s == STEPS - 1:
                        pe.wait_ge(pv_ready, t + 1)
                        pe.matmul(rep_p, rep[:], pv[:], start=True, stop=True).then_inc(rep_done, 1)
                    if p1 and s == NCH:
                        conv1(n, nxt, 0)
                    if p2 and (s > GRP and s % GRP == 1 or s == NCH):
                        m = NG - 1 if s == NCH else s // GRP - 1
                        pe.wait_ge(sqx_done, NCH * b + GRP * (m + 1))
                        sum_group(st2[:, SUB:2 * SUB], sqx[:].rearrange("p g n -> p (g n)"), m, False).then_inc(grp_done, 1)
                    if p1 and s in SUMX_AT:
                        if s == 0:
                            wait(pe, w1n_ready, 2 * n)
                            if tl:
                                pe.wait_ge(idx_ready, t + 1)
                        for m in SUMX_AT[s]:
                            pe.wait_ge(x_in[m], 32 * (n + 1))
                            mm = sum_group(st1[:, 0:SUB], xs[nxt][:], m, True)
                        if m == NG - 1:
                            mm.then_inc(sumx_done, 1)

            def pool_rows(b0, b1):
                for b in range(b0, b1):
                    for g in range(GATHERS):
                        mm = pe.matmul(pc[0:C, NE * b:NE * b + NE], zs[:, b, g, :], esel[:],
                                       start=(g == 0), stop=(g == GATHERS - 1))
                mm.then_inc(pool_done, 1)

            def spread_pixels(p):
                pe.wait_ge(diag_ready, p + 1)
                wait(pe, eq_ready, p - 1)
                pe.matmul(bc[p % 2][:], ones[:], diags[p], start=True, stop=True).then_inc(pxr_done, 1)

            pe.wait_ge(const_v, 1)
            iteration(-1, 1, True, False, False)
            pe.wait_ge(w_in, 16 * 15)
            pe.matmul(pe_b[:, 0:C], cen[:], gbd[:], start=True, stop=True).then_inc(const_t, 1)
            pe.wait_ge(const_v, 3)
            iteration(0, 0, True, True, False)
            with pe.Fori(0, 3) as i:
                iteration(2 * i + 1, 1, True, True, True)
                iteration(2 * i + 2, 0, True, True, True)
            iteration(7, 1, False, True, True)
            iteration(8, 0, False, False, True)
            spread_pixels(3)

            pe.wait_ge(z_ready, 2)
            pool_rows(6, NB)
            pe.wait_ge(pooled_ready, 1)
            for e in range(NE):
                grp, slot = e // 4, e % 4
                mm = pe.matmul(h_banks[grp // 2][32 * slot:32 * slot + 32, HID * (grp % 2):HID * (grp % 2) + HID],
                               pool_f[:, NB * e:NB * e + 32], ew1[:, e, :], start=True, stop=True, skip_group_check=True)
                if e % 8 == 7:
                    mm.then_inc(l1_done, 1)
            for i in range(4):
                pe.wait_ge(gelu_done, i + 1)
                if i == 3:
                    pe.wait_ge(eq_ready, 4)
                for k in range(4):
                    mm = pe.transpose(t_banks[i][:, P * k:P * k + P], hg[:, CH * i + P * k:CH * i + P * k + P], ident[:])
                mm.then_inc(t2_done, 1)
            for e in range(0, NE, 2):
                if e % 8 == 0:
                    pe.wait_ge(ht_ready, e // 8 + 1)
                for k in range(2):
                    for par in range(2):
                        col = 32 * (2 * (e // 4) + k) + NB * ((e + par) % 4)
                        mm = pe.matmul(pd[C * par:C * par + C, NB * (e // 2):NB * (e // 2) + NB], ew2[:, e + par, k, :],
                                       ht[:, col:col + NB], start=(k == 0), stop=(k == 1), skip_group_check=True)
            mm.then_inc(l2_done, 1)
            pe.wait_ge(eo_ready, 1)

            def expert_rows(half):
                for i, b in enumerate(ORDER[4 * half:4 * half + 4]):
                    mm = pe.matmul((pe_b, pd)[half][:, C * i:C * i + C], eot[:, P * b:P * b + P], id2[:], start=True, stop=True)
                mm.then_inc(ob_done, 1)

            def add_rows(i):
                b = ORDER[i]
                pe.wait_ge(z_done, i + 1)
                wait(pe, row_ready, i - 1)
                for g in range(GATHERS):
                    col = GATHERS * C * (i // 2) + C * g
                    for f in range(GATHERS):
                        mm = pe.matmul(add_banks[i % 2][:, col:col + C], eq[:, b, f, P * g:P * g + P], zc[:, b, f, :],
                                       start=(f == 0), stop=(f == GATHERS - 1))
                mm.then_inc(add_done, 1)

            pe.wait_ge(eq_ready, 4)
            expert_rows(0)
            for i in range(NB):
                if i == 2:
                    expert_rows(1)
                add_rows(i)

        @block.scalar
        def _(act):
            def rsqrt_start(v, ln, y, eps, ln_done, y_ready, count):
                nc.scalar.activation(ln, v, ACT.Ln, bias=eps).then_inc(ln_done, 1)
                act.wait_ge(ln_done, count)
                nc.scalar.activation(y, ln, ACT.Exp, scale=-0.5).then_inc(y_ready, 1)

            def token_rsqrt(part, b0, b1):
                act.wait_ge(rvar_ready, part + 1)
                n = slice(GATHERS * b0, GATHERS * b1)
                rsqrt_start(tr[:, 1, n], tr[:, 3, n], tr[:, 2, n], 0.0, rln_done, ry_ready, part + 1)

            def iteration(it, par, p1, p2, tl):
                b, n, t = it, it + 1, it - 1
                nxt = 1 - par

                def relu(b, par, s):
                    act.wait_ge(c_done, NCH * b + s + 1)
                    wait(act, d_done, NCH * b + s - 1)
                    if s == 0:
                        act.wait_ge(w1n_ready, 2 * (b + 1))
                    nc.scalar.activation(hid[s % 2][:], pc[:], ACT.Relu, bias=b1n[:, par:par + 1]).then_inc(h_done, 1)

                def square_xc(k):
                    used(act, it, "C", k, p1, tl)
                    wait(act, sumsq_done, NG * n + k // GRP)
                    nc.scalar.activation(sqc[:, k % GRP, :], chunk(us[nxt], k), ACT.Square).then_inc(sqc_done, 1)

                def square_u(k):
                    used(act, it, "S", k, p1, tl)
                    wait(act, usq_done, NCH * n + k - 1)
                    if k == 0:
                        wait(act, gnred_ready, 2 * n)
                    nc.scalar.activation(junk[:, k % 2, :], chunk(us[nxt], k), ACT.Square,
                                         accum_out=gsq[:, k:k + 1]).then_inc(usq_done, 1)

                for s in range(STEPS):
                    if p2 and s + 1 < NCH:
                        relu(b, par, s + 1)
                    if p2 and s >= 1:
                        act.wait_ge(e_done, NCH * b + s)
                        j = chunk_of(s - 1)
                        nc.scalar.activation(lg[par][:, SUB * j:SUB * (j + 1)], lgp, ACT.Copy).then_inc(lcopy_done, 1)
                        act.wait_ge(t_done, NCH * b + s)
                        wait(act, stored[(s - 1) % 2], 16 * (8 * b + (s - 1) // 2))
                        nc.scalar.activation(tok[(s - 1) % 2][:].rearrange("p h t c -> p t h c"),
                                             pt[:].rearrange("p (t h c) -> p t h c", t=4, h=2), ACT.Copy).then_inc(tok_done, 1)
                    if p1:
                        for k in C_AT.get(s, ()):
                            square_xc(k)
                        for k in S_AT.get(s, ()):
                            square_u(k)
                    if tl and s == 0:
                        act.wait_ge(grp_done, NG * (t + 1))
                        nc.scalar.activation(ta[:], st2[:, 0:SUB], ACT.Square).then_inc(msq_done, 1)
                        act.wait_ge(var2_ready, t + 1)
                        rsqrt_start(v2[:], ta[:], y2[:], 0.0, ln2_done, y2_ready, t + 1)
                    if p1 and s == RSTD_AT:
                        act.wait_ge(sumsq_done, NG * (n + 1))
                        act.wait_ge(const_v, 2)
                        nc.scalar.activation(lnv[:], st1[:, SUB:2 * SUB], ACT.Ln, bias=gt[:, 10:11]).then_inc(lnv_done, 1)
                        act.wait_ge(lnv_done, n + 1)
                        nc.scalar.activation(y0[:], lnv[:], ACT.Exp, scale=-0.5).then_inc(y0_ready, 1)
                    if tl and s in EXP_AT:
                        i = EXP_AT[s]
                        act.wait_ge(top_ready, PIECES * t + i + 1)
                        nc.scalar.activation(piece(lg[nxt], i), piece(lg[nxt], i), ACT.Exp, bias=nmax[:, i:i + 1],
                                             accum_out=cnd[:, 2 * CAND + i:2 * CAND + i + 1]).then_inc(expl_done, 1)
                    if p2 and not p1 and s == NORM_AT[1]:
                        token_rsqrt(0, 0, 6)
                    if tl and s == MERGE_AT + 2:
                        act.wait_ge(bias_ready, t + 1)
                        nc.scalar.activation(tval[:], fval[:], ACT.Exp, bias=gbm[:, 1:2]).then_inc(tval_done, 1)
                        nc.scalar.activation(dexp[:], cval[:, 0:4 * CAND:K], ACT.Exp, bias=gbm[:, 1:2]).then_inc(tval_done, 1)
                    if p1 and s == GN_AT + 2:
                        act.wait_ge(gnv_ready, n + 1)
                        rsqrt_start(gt[:, 3:4], gt[:, 8:9], gt[:, 4:5], 0.0, gnln_done, gny_ready, n + 1)
                    if p1 and s == NCH:
                        relu(n, nxt, 0)

            nc.scalar.preload_act_table_set("natural_log_exp_and_others")
            iteration(-1, 1, True, False, False)
            iteration(0, 0, True, True, False)
            with act.Fori(0, 3) as i:
                iteration(2 * i + 1, 1, True, True, True)
                iteration(2 * i + 2, 0, True, True, True)
            iteration(7, 1, False, True, True)
            iteration(8, 0, False, False, True)

            token_rsqrt(1, 6, NB)
            nc.scalar.preload_act_table_set("gelu_and_others")
            for i in range(4):
                act.wait_ge(l1_done, i + 1)
                nc.scalar.activation(hg[:, CH * i:CH * i + CH], h_banks[i][:], ACT.Gelu).then_inc(gelu_done, 1)

        @block.vector
        def _(dve):
            def iteration(it, par, p1, p2, tl):
                b, n, t = it, it + 1, it - 1
                nxt = 1 - par
                tail = Steps(dve, tail_steps, TAIL_STEPS * t if tl else 0)

                def pix(i):
                    return cnd[:, CAND + K * i:CAND + K * (i + 1)]

                def use_spread(job, i):
                    kind, k = job
                    dve.wait_ge(bc_filled[i % 2], spread_pairs(it) + i // 2 + 1)
                    stat = bc[i % 2][:]
                    if kind == "L":
                        if k == 0:
                            dve.wait_ge(lcopy_done, NCH * (t + 1))
                        lt = lg[nxt][:, CH * k:CH * (k + 1)]
                        ins = nc.vector.tensor_tensor(lt, lt, stat, ALU.mult)
                    elif kind == "C":
                        ins = nc.vector.tensor_tensor(chunk(us[nxt], k), chunk(xs[nxt], k), stat, ALU.subtract)
                    else:
                        ins = nc.vector.tensor_tensor_reduce(chunk(us[nxt], k), chunk(us[nxt], k), stat, 1.0, 0.0,
                                                             ALU.mult, ALU.add, gsum[:, k:k + 1])
                    ins.then_inc(bc_used[i % 2], 1)

                for s in range(STEPS):
                    jobs, before = spreads(s, p1, tl)
                    jobs = [(job, before + i) for i, job in enumerate(jobs)]
                    if p1 and s == MEAN_AT:
                        link = Steps(dve, mean_steps, MEAN_STEPS * n)
                        dve.wait_ge(sumx_done, n + 1)
                        link(nc.vector.tensor_copy(hi[:], st1[:, 0:SUB]))
                        nc.vector.scalar_tensor_tensor(out=mean_s[:], in0=hi[:].bitcast(F32), scalar=second[:], in1=st1[:, 0:SUB],
                                                       op0=ALU.mult, op1=ALU.add).then_inc(mean_ready, 1)
                    if p1 and s == RSTD_AT + 1:
                        link = Steps(dve, rstd_steps, RSTD_STEPS * n)
                        dve.wait_ge(y0_ready, n + 1)
                        newton(link, st1[:, SUB:2 * SUB], y0[:], tb[:], EPS_C)
                        link(nc.vector.scalar_tensor_tensor(out=tb[:], in0=tb[:], scalar=1.5, in1=y0[:], op0=ALU.add, op1=ALU.mult))
                        link(nc.vector.tensor_copy(hi[:], tb[:]))
                        nc.vector.scalar_tensor_tensor(out=rstd_s[:], in0=hi[:].bitcast(F32), scalar=second[:], in1=tb[:],
                                                       op0=ALU.mult, op1=ALU.add).then_inc(rstd_ready, 1)
                    if p1 and s == GN_AT + 1:
                        dve.wait_ge(usq_done, NCH * (n + 1))
                        nc.vector.tensor_reduce(gs[:, 1:2], gsq[:], AX.X, ALU.add).then_inc(gnred_ready, 1)
                    if p1 and s == GN_AT + 2:
                        link = Steps(dve, gn_steps, GN_STEPS * n)
                        dve.wait_ge(gnps_done, 2 * n + 1)
                        link(nc.vector.tensor_copy(gt[:, 0:2], gn_p))
                        link(nc.vector.scalar_tensor_tensor(out=gt[:, 2:3], in0=gt[:, 0:1], scalar=gt[:, 0:1], in1=gt[:, 1:2],
                                                            op0=ALU.mult, op1=ALU.subtract))
                        link(nc.vector.tensor_scalar(gt[:, 2:3], gt[:, 2:3], -1.0, EPS, ALU.mult, ALU.add))
                        nc.vector.tensor_scalar(gt[:, 3:4], gt[:, 2:3], EPS, None, ALU.max).then_inc(gnv_ready, 1)
                    if tl and s == 0:
                        dve.wait_ge(msq_done, t + 1)
                        tail(nc.vector.scalar_tensor_tensor(out=v2[:], in0=st2[:, SUB:2 * SUB], scalar=EPS, in1=ta[:],
                                                            op0=ALU.add, op1=ALU.subtract))
                        nc.vector.tensor_scalar(v2[:], v2[:], EPS, None, ALU.max).then_inc(var2_ready, 1)
                    for job in jobs[:first(jobs)]:
                        use_spread(*job)
                    if p2 and s < NCH:
                        dve.wait_ge(d_done, NCH * b + s + 1)
                        dve.wait_ge(s_done, NCH * b + s + 1)
                        xc = chunk(xs[par], s)
                        nc.vector.scalar_tensor_tensor(out=xc, in0=pd[:], scalar=vecs[:, 3:4], in1=xc,
                                                       op0=ALU.add, op1=ALU.add).then_inc(x1_done, 1)
                    for job in jobs[first(jobs):]:
                        use_spread(*job)
                    if tl and s == 0:
                        dve.wait_ge(y2_ready, t + 1)
                        newton(tail, v2[:], y2[:], tb[:], 0.0)
                        tail(nc.vector.scalar_tensor_tensor(out=tb[:], in0=tb[:], scalar=1.5, in1=y2[:], op0=ALU.add, op1=ALU.mult))
                        tail(nc.vector.tensor_copy(hi[:], tb[:]))
                        nc.vector.scalar_tensor_tensor(out=rstd2_s[:], in0=hi[:].bitcast(F32), scalar=second[:], in1=tb[:],
                                                       op0=ALU.mult, op1=ALU.add).then_inc(rstd2_ready, 1)
                    if tl and s in MAX_AT:
                        i = MAX_AT[s]
                        for k in (2 * i, 2 * i + 1):
                            used(dve, it, "L", k, p1, tl)
                        hold(dve, spare[:, 0:1])
                        tail(nc.vector.max(cnd[:, K * i:K * i + K], piece(lg[nxt], i)))
                    if tl and s in FIND_AT:
                        i = FIND_AT[s]
                        hold(dve, spare[:, 0:1])
                        tail(nc.vector.max_index(top_i[:], cnd[:, K * i:K * i + K], piece(lg[nxt], i)))
                        nc.vector.tensor_scalar(nmax[:, i:i + 1], cnd[:, K * i:K * i + 1], -1.0, None, ALU.mult)
                        tail(nc.vector.tensor_scalar(top_hi[:], top_i[:], 0xFFFFFF00, None, ALU.bitwise_and))
                        tail(nc.vector.scalar_tensor_tensor(out=pix(i), in0=top_i[:], scalar=rowoff[:], in1=top_hi[:],
                                                            op0=ALU.add, op1=ALU.add))
                        nc.vector.tensor_scalar(pix(i), pix(i), float(2 * PIECE * i), None, ALU.add).then_inc(top_ready, 1)
                    if p2 and not p1 and s == 0:
                        nc.vector.tensor_copy(idx_all[:, LOOPED:LOOPED + 1, :], px_all[:, LOOPED:LOOPED + 1, :]).then_inc(late_ready, 1)
                    if p2 and not p1 and s == 2:
                        nc.vector.memset(ones[:], 1.0)
                    if tl and s == MERGE_AT + 1:
                        dve.wait_ge(mrg_done, t + 1)
                        m4 = mrg_p.rearrange("e (r k) -> e r k", r=4)
                        nc.vector.tensor_copy(cpix[:].rearrange("e (r k) -> e r k", r=4), m4[:, :, CAND:2 * CAND])
                        nc.vector.tensor_copy(csum[:].rearrange("e (r k) -> e r k", r=4), m4[:, :, 2 * CAND:])
                        tail(nc.vector.tensor_copy(cval[:].rearrange("e (r k) -> e r k", r=4), m4[:, :, 0:CAND]))
                        hold(dve, spare[:, 0:1])
                        tail(nc.vector.max(fval[:], cval[:]))
                        hold(dve, spare[:, 0:1])
                        tail(nc.vector.max_index(fpos[:], fval[:], cval[:]))
                        tail(nc.vector.tensor_tensor(gbm[:, 0:1], fval[:, 0:1], gate_bias[:], ALU.add))
                        nc.vector.tensor_tensor(gbm[:, 1:2], gate_bias[:], gbm[:, 0:1], ALU.subtract).then_inc(bias_ready, 1)
                        tail(nc.vector.tensor_copy(fposf[:], fpos[:]))

                    def pixels(half):
                        ks = slice(K // 2 * half, K // 2 * (half + 1))
                        onehot = onehots[p1]
                        shape = [NE, K // 2, 4 * CAND]
                        tail(nc.vector.tensor_tensor(onehot, iota[:].unsqueeze(1).broadcast_to(shape),
                                                     fposf[:, ks].unsqueeze(2).broadcast_to(shape), ALU.is_equal))
                        tail(nc.vector.tensor_tensor(onehot, onehot, cpix[:].unsqueeze(1).broadcast_to(shape), ALU.mult))
                        tail(nc.vector.tensor_reduce(pv[:, ks], onehot, AX.X, ALU.add))

                    if p2 and not p1 and s in NORM_AT:
                        token_norm(0, 0, 6, (NORM_AT.index(s),))
                    if p2 and not p1 and s in PAIR_AT:
                        equal_pixels(PAIR_AT.index(s))
                    if p2 and not p1 and s + 1 in PAIR_AT:
                        diagonals(PAIR_AT.index(s + 1))
                    if not p1 and not p2 and s == 0:
                        lns(nc.vector.tensor_tensor(id2[:], ident[:, 0:C], ident[:, C:P], ALU.add))
                    if p1 and s == GN_AT:
                        for k in (NCH - 2, NCH - 1):
                            used(dve, it, "S", k, p1, tl)
                        nc.vector.tensor_reduce(gs[:, 0:1], gsum[:], AX.X, ALU.add).then_inc(gnred_ready, 1)
                    if p1 and s == GN_AT + 2:
                        dve.wait_ge(gny_ready, n + 1)
                        newton(link, gt[:, 3:4], gt[:, 4:5], gt[:, 5:6], 0.0)
                        link(nc.vector.scalar_tensor_tensor(out=gt[:, 5:6], in0=gt[:, 5:6], scalar=1.5, in1=gt[:, 4:5],
                                                            op0=ALU.add, op1=ALU.mult))
                        link(nc.vector.tensor_tensor(gt[:, 6:7], vecs[:, 0:1], gt[:, 5:6], ALU.mult))
                        nc.vector.scalar_tensor_tensor(out=gt[:, 7:8], in0=gt[:, 0:1], scalar=gt[:, 6:7], in1=vecs[:, 1:2],
                                                       op0=ALU.mult, op1=ALU.subtract).then_inc(gnbias_ready, 1)
                        nc.vector.tensor_scalar(w1n[nxt][:], w1bd[:], gt[:, 6:7], None, ALU.mult).then_inc(w1n_ready, 1)
                        assert link.n == GN_STEPS, link.n
                    if tl and s == GN_AT:
                        pixels(0)
                    if tl and s == GN_AT + 1:
                        pixels(1)
                    if tl and s == GN_AT + 2:
                        dve.wait_ge(tval_done, 2 * (t + 1))
                        tail(nc.vector.tensor_tensor_reduce(djunk[:], dexp[:], csum[:], 1.0, 0.0, ALU.mult, ALU.add, gbm[:, 2:3]))
                        tail(nc.vector.reciprocal(gbm[:, 3:4], gbm[:, 2:3]))
                        nc.vector.tensor_scalar(pv[:, K:2 * K], tval[:], gbm[:, 3:4], None, ALU.mult).then_inc(pv_ready, 1)
                    if p1 and s == GN_AT + 3:
                        if tl:
                            dve.wait_ge(rep_done, t + 1)
                        dve.wait_ge(gnps_done, 2 * n + 2)
                        nc.vector.tensor_tensor(b1n[:, nxt:nxt + 1], vecs[:, 2:3], gnb_p, ALU.subtract).then_inc(w1n_ready, 1)
                    if tl and s == STEPS - 1:
                        dve.wait_ge(rep_done, t + 1)
                        tail(nc.vector.tensor_tensor(pvm[:], kmask[:].unsqueeze(1).broadcast_to([P, 2 * GATHERS, 4]),
                                                     rep_p.rearrange("p (a k) -> p a k", k=4), ALU.mult))
                        tail(nc.vector.tensor_reduce(pvt[:], pvm[:], AX.X, ALU.add))
                        tail(nc.vector.tensor_scalar(idxf[:], pvt[:, 0:GATHERS], 0.0 if isinstance(it, int) else offs[:],
                                                     None, ALU.add))
                        at = slice(t, t + 1) if isinstance(t, int) else bass.ds(t, 1)
                        nc.vector.tensor_copy(idx_all[:, at, :], idxf[:].unsqueeze(1))
                        nc.vector.tensor_copy(px_all[:, at, :], pvt[:, 0:GATHERS].unsqueeze(1))
                        tail(nc.vector.tensor_copy(tv_all[:, at, :], pvt[:, GATHERS:].unsqueeze(1)))
                        nc.vector.tensor_scalar(offs[:], offs[:], float(PIX * (1 - par)), None, ALU.add).then_inc(idx_ready, 1)
                        assert tail.n == TAIL_STEPS, tail.n

            lns = Steps(dve, ln_steps, 0)

            def token_norm(part, b0, b1, stages=(0, 1, 2)):
                n0, n1 = GATHERS * b0, GATHERS * b1
                shape = [P, n1 - n0, C]
                r = rows_all.rearrange("p b g c -> p (b g) c")[:, n0:n1]
                zz = zs.rearrange("p b g c -> p (b g) c")[:, n0:n1]
                q = zsq[part][:, 0:(n1 - n0) * C].rearrange("p (n c) -> p n c", c=C)
                mean, var, y, a, rs, ws = (tr[:, i, n0:n1] for i in range(6))
                if 0 in stages:
                    dve.wait_ge(rows_in[part], 16 * GATHERS * (b1 - b0))
                    lns(nc.vector.tensor_reduce(mean, r, AX.X, ALU.add))
                    lns(nc.vector.tensor_scalar(mean, mean, 1.0 / C, None, ALU.mult))
                    lns(nc.vector.tensor_tensor(zz, r, mean.unsqueeze(2).broadcast_to(shape), ALU.subtract))
                if 1 in stages:
                    lns(nc.vector.tensor_tensor(q, zz, zz, ALU.mult))
                    lns(nc.vector.tensor_reduce(var, q, AX.X, ALU.add))
                    nc.vector.tensor_scalar(var, var, 1.0 / C, EPS, ALU.mult, ALU.add).then_inc(rvar_ready, 1)
                if 2 in stages:
                    dve.wait_ge(ry_ready, part + 1)
                    newton(lns, var, y, a, 0.0)
                    lns(nc.vector.scalar_tensor_tensor(out=rs, in0=a, scalar=1.5, in1=y, op0=ALU.add, op1=ALU.mult))
                    lns(nc.vector.tensor_tensor(ws, rs, tv_all[:, b0:b1].rearrange("p b g -> p (b g)"), ALU.mult))
                    nc.vector.tensor_tensor(zz, zz, ws.unsqueeze(2).broadcast_to(shape), ALU.mult).then_inc(z_ready, 1)

            def diagonals(p):
                pairs = px_all[:, 2 * p:2 * p + 2, :].rearrange("p b g -> p (b g)")
                shape = [P, 2 * GATHERS, P]
                nc.vector.tensor_tensor(diags[p].rearrange("p (n i) -> p n i", i=P), ident[:].unsqueeze(1).broadcast_to(shape),
                                        pairs.unsqueeze(2).broadcast_to(shape), ALU.mult).then_inc(diag_ready, 1)

            def equal_pixels(p):
                dve.wait_ge(pxr_done, p + 1)
                for i, b in enumerate((2 * p, 2 * p + 1)):
                    for f in range(GATHERS):
                        ins = nc.vector.tensor_scalar(eq[:, b, f, :], bc[p % 2][:, SUB * i:SUB * i + SUB],
                                                      px_all[:, b, f:f + 1], None, ALU.is_equal)
                ins.then_inc(eq_ready, 1)
                dve.wait_ge(eq_ready, p + 1)

            cv = Steps(dve, const_steps, 0)
            nc.vector.memset(w1bd[:], 0.0)
            nc.vector.memset(w2bd[:], 0.0)
            nc.vector.memset(gbd[:], 0.0).then_inc(const_d, 1)
            for r in range(4):
                nc.vector.memset(rowoff[32 * r:32 * r + 32, :], float(SUB * (r // 2) + HW * (r % 2)))
            nc.vector.memset(offs[:], 0.0).then_inc(idx_ready, 1)
            nc.vector.memset(gt[:, 10:11], EPS_C)
            cv(nc.vector.memset(stat_w[:], 0.0))
            sw = stat_w[:].rearrange("p q m -> p (q m)")
            for h in range(HALVES):
                for d in range(2):
                    ins = nc.vector.memset(sw[C * h:C * h + C, h + 16 * d:h + 16 * d + 34 * 7 + 1:34], 1.0 / C)
            ins.then_inc(const_v, 1)
            dve.wait_ge(const_p, 1)
            for q in range(4):
                r = slice(32 * q, 32 * q + 32)
                lo, up = (ident[r, 32 * q + 16 * i:32 * q + 16 * (i + 1)] for i in range(2))
                nc.vector.tensor_tensor(tb[r, 0:16], lo, up, ALU.add)
                cv(nc.vector.tensor_reduce(tb[r, 16:17], up, AX.X, ALU.add))
            nc.vector.tensor_copy(spread[:].rearrange("p (r y) -> p r y", y=C), tb[:, 0:16].unsqueeze(2).broadcast_to([P, 16, C]))
            nc.vector.tensor_scalar(second[:], tb[:, 16:17], -1.0, None, ALU.mult)
            nc.vector.tensor_copy(rep[:].rearrange("e (k f) -> e k f", k=4),
                                  ident[0:NE, 0:NE].unsqueeze(1).broadcast_to([NE, 4, NE]))
            nc.vector.tensor_reduce(kmask[:], ident[:].rearrange("p (k e) -> p k e", k=4), AX.X, ALU.add)
            cv(nc.vector.tensor_reduce(esel[:], ident[:].rearrange("p (k e) -> p e k", k=4), AX.X, ALU.add))
            cv(nc.vector.memset(cen[:], 0.0))
            for h in range(HALVES):
                ins = nc.vector.memset(cen[C * h:C * h + C, C * h:C * h + C], 1.0 / C)
            cv(ins)
            nc.vector.tensor_tensor(cen[:], ident[:], cen[:], ALU.subtract).then_inc(const_v, 1)
            dve.wait_ge(const_v, 2)

            iteration(-1, 1, True, False, False)
            dve.wait_ge(const_t, 1)
            nc.vector.tensor_copy(gcen[:], pe_b[:, 0:C]).then_inc(const_v, 1)
            iteration(0, 0, True, True, False)
            with dve.Fori(0, 3) as i:
                iteration(2 * i + 1, 1, True, True, True)
                iteration(2 * i + 2, 0, True, True, True)
            iteration(7, 1, False, True, True)
            iteration(8, 0, False, False, True)

            diagonals(3)
            dve.wait_ge(pex_done, 1)
            nc.vector.tensor_copy(eb2t, pt[:, 0:NE]).then_inc(ebias_ready, 1)
            token_norm(1, 6, NB)
            dve.wait_ge(zero_ready, 1)
            dve.wait_ge(pool_done, 2)
            nc.vector.tensor_copy(pool_f[0:C, 0:NE * NB].rearrange("c (e b) -> c b e", b=NB),
                                  pc[0:C, 0:NE * NB].rearrange("c (b e) -> c b e", b=NB)).then_inc(pooled_ready, 1)
            equal_pixels(3)
            for i in range(4):
                dve.wait_ge(t2_done, i + 1)
                nc.vector.tensor_copy(ht[:, P * i:P * i + P].rearrange("p (a b) -> p a b", b=NB),
                                      t_banks[i][:].rearrange("p (a r) -> p a r", r=32)[:, :, 0:NB]).then_inc(ht_ready, 1)
            dve.wait_ge(l2_done, 1)
            dve.wait_ge(ebias_ready, 1)
            for par in range(2):
                rows, shape = slice(C * par, C * par + C), [C, 4, NE // 2, NB]
                ins = nc.vector.tensor_tensor(
                    eot[rows].rearrange("o (b k e) -> o k e b", b=NB, k=4)[:, :, par:NE:2, :],
                    eb2t[rows, par:NE:2].unsqueeze(1).unsqueeze(3).broadcast_to(shape),
                    pd[rows, 0:NE // 2 * NB].rearrange("o (e b) -> o e b", b=NB).unsqueeze(1).broadcast_to(shape), ALU.add)
            ins.then_inc(eo_ready, 1)

            def contributions(half):
                dve.wait_ge(ob_done, half + 1)
                shape = [P, GATHERS, C]
                for i, b in enumerate(ORDER[4 * half:4 * half + 4]):
                    nc.vector.tensor_tensor(zc[:, b], (pe_b, pd)[half][:, C * i:C * i + C].unsqueeze(1).broadcast_to(shape),
                                            tv_all[:, b].unsqueeze(2).broadcast_to(shape), ALU.mult).then_inc(z_done, 1)

            def result_rows(i):
                dve.wait_ge(add_done, i + 1)
                rv = rows_all[:, ORDER[i]].rearrange("p g c -> p (g c)")
                col = GATHERS * C * (i // 2)
                nc.vector.tensor_tensor(rv, rv, add_banks[i % 2][:, col:col + GATHERS * C], ALU.add).then_inc(row_ready, 1)

            contributions(0)
            for i in range(NB):
                result_rows(i)
                if i == 1:
                    contributions(1)

        @block.gpsimd
        def _(pool):
            cp = Steps(pool, pool_steps, 0)
            cp(nc.gpsimd.memset(ident[:], 0.0))
            nc.gpsimd.affine_select(out=ident[:], in_=ident[:], compare_op=ALU.not_equal, fill=1.0, base=0,
                                    pattern=[[-1, P]], channel_multiplier=1).then_inc(const_p, 1)
            nc.gpsimd.iota(iota[:], pattern=[[1, 4 * CAND]], base=0, channel_multiplier=0, allow_small_or_imprecise_dtypes=True)
            cp(nc.gpsimd.memset(gsel[:], 1.0 / (GN_GROUP * PIX)))
            for h in range(HALVES):
                v = gsel[C * h:C * h + C, :].rearrange("p (a g i) -> p a g i", a=2, g=C // GN_GROUP)
                pat = [[0, 2], [-GN_GROUP, C // GN_GROUP], [0, GN_GROUP]]
                cp(nc.gpsimd.affine_select(out=v, in_=v, compare_op=ALU.is_ge, fill=0.0, base=0, pattern=pat,
                                           channel_multiplier=1))
                pat = [[0, 2], [GN_GROUP, C // GN_GROUP], [0, GN_GROUP]]
                ins = nc.gpsimd.affine_select(out=v, in_=v, compare_op=ALU.is_ge, fill=0.0, base=GN_GROUP - 1, pattern=pat,
                                              channel_multiplier=-1)
            ins.then_inc(const_p, 1)

            def gather(b):
                last = max(b, LOOPED - 1)
                for q in range(2):
                    pool.wait_ge(stored[q], 16 * (NCH // 2) * (last + 1))
                pool.wait_ge(idx_ready, last + 2)
                pool.wait_ge(late_ready, 1)
                for g in range(GATHERS):
                    nc.gpsimd.indirect_dma_start(
                        rows_all[:, b, g, :], None, out_rows[place(b)[0]],
                        bass.IndirectOffsetOnAxis(ap=idx_all[:, b, g:g + 1], axis=0)).then_inc(rows_in[b >= 6], 16)

            def iteration(it, par, p1, p2, tl):
                b, n, t = it, it + 1, it - 1
                nxt = 1 - par
                for s in range(STEPS):
                    if p2 and not p1 and 1 <= s <= 6:
                        gather(s - 1)
                    if not p1 and not p2 and s == 0:
                        pool.wait_ge(idx_ready, NB)
                        pool.wait_ge(h_done, NCH * NB)
                        nc.gpsimd.memset(pool_f, 1.0)
                        nc.gpsimd.memset(eot, 0.0).then_inc(zero_ready, 1)
                    if p2 and s in LATE_ADD_AT:
                        k = LATE_ADD_AT[s]
                        pool.wait_ge(w1n_ready, 2 * (b + 1))
                        nc.gpsimd.tensor_tensor(chunk(xs[par], k), chunk(xs[par], k), chunk(us[par], k),
                                                ALU.add).then_inc(s_done, 1)
                    if p2 and s < NCH:
                        pool.wait_ge(x1_done, NCH * b + s + 1)
                        wait(pool, grp_done, NG * b + s // GRP)
                        xc = chunk(xs[par], s)
                        nc.gpsimd.tensor_tensor(sqx[:, s % GRP, :], xc, xc, ALU.mult).then_inc(sqx_done, 1)
                    if p1:
                        for k in ADD_AT.get(s, ()):
                            used(pool, it, "S", k, p1, tl)
                            nc.gpsimd.tensor_tensor(chunk(xs[nxt], k), chunk(xs[nxt], k), chunk(us[nxt], k),
                                                    ALU.add).then_inc(s_done, 1)
            pool.wait_ge(const_p, 2)
            iteration(-1, 1, True, False, False)
            iteration(0, 0, True, True, False)
            with pool.Fori(0, 3) as i:
                iteration(2 * i + 1, 1, True, True, True)
                iteration(2 * i + 2, 0, True, True, True)
            iteration(7, 1, False, True, True)
            iteration(8, 0, False, False, True)
            gather(6)
            gather(7)
            before = [0] * len(outs)
            for b, g in SCATTERS:
                pool.wait_ge(row_ready, ORDER.index(b) + 1)
                q = place(b)[0]
                wait(pool, scattered[q], 16 * before[q])
                nc.gpsimd.indirect_dma_start(
                    out_rows[q], bass.IndirectOffsetOnAxis(ap=idx_all[:, b, g:g + 1], axis=0),
                    rows_all[:, b, g, :], None).then_inc(scattered[q], 16)
                before[q] += 1
            for q in range(len(outs)):
                pool.wait_ge(scattered[q], 16 * before[q])


def kernel(x, L0_conv_gn_w, L0_conv_gn_b, L0_conv_w1, L0_conv_b1, L0_conv_w2, L0_conv_b2,
           L0_ffn_gate_w, L0_ffn_gate_b, L0_ffn_weight1, L0_ffn_weight2):
    import numpy as np
    import concourse.bacc as bacc
    from concourse.bass_utils import run_bass_kernel_spmd

    ins = {
        "x": np.ascontiguousarray(x).reshape(NB, C, PIX),
        "gn_w": L0_conv_gn_w, "gn_b": L0_conv_gn_b,
        "w1T": np.asarray(L0_conv_w1).T, "b1": L0_conv_b1,
        "w2T": np.asarray(L0_conv_w2).T, "b2": L0_conv_b2,
        "gateT": np.asarray(L0_ffn_gate_w).T, "gate_b": L0_ffn_gate_b,
        "e_w1": L0_ffn_weight1, "e_w2": L0_ffn_weight2,
    }
    nc = bacc.Bacc("TRN2", target_bir_lowering=False, num_devices=1)
    arrays, args = {}, []
    for name, a in ins.items():
        a = np.ascontiguousarray(a)
        arrays[f"in_{name}"] = a
        args.append(nc.dram_tensor(f"in_{name}", a.shape, mybir.dt.from_np(a.dtype), kind="ExternalInput").ap())
    places = [place(b) for b in range(NB)]
    names = [f"out_rows{q}" for q in range(max(q for q, _ in places) + 1)]
    for q, name in enumerate(names):
        count = sum(p[0] == q for p in places)
        args.append(nc.dram_tensor(name, (count, PIX, C), F32, kind="ExternalOutput").ap())
    mk_metaformer_kernel(nc, *args)
    r = run_bass_kernel_spmd(nc, [arrays], core_ids=[0])
    got = np.stack([r.results[0][names[q]][at] for q, at in places])
    return np.ascontiguousarray(got.transpose(0, 2, 1)).reshape(NB, C, 128, 128)
```
